# Optimizing a Trainium2 kernel written in Bass

```python
import numpy as np
import jax
import jax.numpy as jnp

def _softmax(x, axis=-1):
    return jax.nn.softmax(x, axis=axis)

def _gelu(x):
    return jax.nn.gelu(x, approximate=True)

def _silu(x):
    return jax.nn.silu(x)

def _sigmoid(x):
    return jax.nn.sigmoid(x)

def _layernorm(x, axis=-1, eps=1e-05):
    m = jnp.mean(x, axis=axis, keepdims=True)
    v = jnp.var(x, axis=axis, keepdims=True)
    return (x - m) / jnp.sqrt(v + eps)

def _scatter_add(tgt, idx, src, axis=0):
    return tgt.at[idx].add(src)

def _segment_sum(src, seg, n):
    return jax.ops.segment_sum(src, seg, n)
kernel_name = 'mk_gnn_ffn_d1_gnn_r8_70b83b'

def setup_inputs(seed: int=0):
    np.random.seed(seed)
    _w = jnp.asarray

    def _rec_inputs():
        import jax
        import jax.numpy as jnp
        _gk = jax.random.key(seed)
        x = -0.0003713 + 1 * jax.random.normal(jax.random.fold_in(_gk, 1), (6250, 256), jnp.float32)
        _s = jax.random.randint(jax.random.fold_in(_gk, 2), (50000,), 0, 6250, jnp.int32)
        _d = jax.random.randint(jax.random.fold_in(_gk, 3), (50000,), 0, 6250, jnp.int32)
        _loop = jnp.arange(6250, dtype=jnp.int32)
        src = jnp.concatenate([_s, _d, _loop])
        dst = jnp.concatenate([_d, _s, _loop])
        _o = jnp.argsort(dst, stable=True)
        src = src[_o]
        dst = dst[_o]
        return (x, src, dst)
    x, src, dst = _rec_inputs()

    def _L0_gnn_setup():
        import jax, jax.numpy as jnp
        import numpy as np
        N_NODES = 6250
        N_EDGES = 200000
        IN_FEATS = 256
        HIDDEN = 512
        OUT_FEATS = 256
        EPS = 0.0
        key = jax.random.key(seed)
        ks = jax.random.split(key, 6)
        x = jax.random.normal(ks[0], (N_NODES, IN_FEATS), dtype=jnp.float32)
        edge_row = jax.random.randint(ks[1], (N_EDGES,), 0, N_NODES, dtype=jnp.int32)
        edge_col = jax.random.randint(ks[2], (N_EDGES,), 0, N_NODES, dtype=jnp.int32)
        W1 = jax.random.uniform(ks[3], (IN_FEATS, HIDDEN), dtype=jnp.float32, minval=-1.0 / np.sqrt(IN_FEATS), maxval=1.0 / np.sqrt(IN_FEATS))
        b1 = jnp.zeros((HIDDEN,), dtype=jnp.float32)
        W2 = jax.random.uniform(ks[4], (HIDDEN, OUT_FEATS), dtype=jnp.float32, minval=-1.0 / np.sqrt(HIDDEN), maxval=1.0 / np.sqrt(HIDDEN))
        b2 = jnp.zeros((OUT_FEATS,), dtype=jnp.float32)
        return {'x': x, 'edge_row': edge_row, 'edge_col': edge_col, 'W1': W1, 'b1': b1, 'W2': W2, 'b2': b2}
    _L0_gnn_all = _L0_gnn_setup()
    _L0_gnn_in = {k: v for k, v in _L0_gnn_all.items() if k in ('W1', 'b1', 'W2', 'b2')}
    del _L0_gnn_all

    def _L0_ffn_setup():
        import jax, jax.numpy as jnp
        import numpy as np
        N_EXPERTS = 8
        TOP_K = 2
        key = jax.random.key(seed)
        ks = jax.random.split(key, 5)
        B, T, C, E, H = (8, 256, 256, 8, 682)
        scale = 1.0 / np.sqrt(C)
        return {'x': jax.random.normal(ks[0], (B, T, C), dtype=jnp.float32), 'router_w': jax.random.normal(ks[1], (E, C), dtype=jnp.float32) * scale, 'w1': jax.random.normal(ks[2], (E, H, C), dtype=jnp.float32) * scale, 'w2': jax.random.normal(ks[3], (E, C, H), dtype=jnp.float32) * (1.0 / np.sqrt(H)), 'w3': jax.random.normal(ks[4], (E, H, C), dtype=jnp.float32) * scale}
    _L0_ffn_all = _L0_ffn_setup()
    _L0_ffn_in = {k: v for k, v in _L0_ffn_all.items() if k in ('router_w', 'w1', 'w2', 'w3')}
    del _L0_ffn_all
    return {'x': x, 'src': src, 'dst': dst, 'L0_gnn_W1': _L0_gnn_in['W1'], 'L0_gnn_b1': _L0_gnn_in['b1'], 'L0_gnn_W2': _L0_gnn_in['W2'], 'L0_gnn_b2': _L0_gnn_in['b2'], 'L0_ffn_router_w': _L0_ffn_in['router_w'], 'L0_ffn_w1': _L0_ffn_in['w1'], 'L0_ffn_w2': _L0_ffn_in['w2'], 'L0_ffn_w3': _L0_ffn_in['w3']}

def reference(x, src, dst, L0_gnn_W1, L0_gnn_b1, L0_gnn_W2, L0_gnn_b2, L0_ffn_router_w, L0_ffn_w1, L0_ffn_w2, L0_ffn_w3):
    import jax
    import jax.numpy as jnp

    def _L0_gnn_ref(x, edge_row, edge_col, W1, b1, W2, b2):
        import jax, jax.numpy as jnp
        import numpy as np
        N_NODES = 6250
        N_EDGES = 200000
        IN_FEATS = 256
        HIDDEN = 512
        OUT_FEATS = 256
        EPS = 0.0
        agg = jax.ops.segment_sum(x[edge_col], edge_row, num_segments=N_NODES)
        h = agg + (1.0 + EPS) * x
        h = h @ W1 + b1
        out = h @ W2 + b2
        return out

    def _L0_ffn_ref(x, router_w, w1, w2, w3):
        import jax, jax.numpy as jnp
        import numpy as np
        N_EXPERTS = 8
        TOP_K = 2
        B, T, C = x.shape
        flat = x.reshape(-1, C)
        logits = flat @ router_w.T
        probs = jax.nn.softmax(logits, axis=-1)
        topk_probs, topk_idx = jax.lax.top_k(probs, TOP_K)
        topk_probs = topk_probs / (jnp.sum(topk_probs, axis=-1, keepdims=True) + 1e-09)
        onehot = jax.nn.one_hot(topk_idx, N_EXPERTS, dtype=flat.dtype)
        gates = jnp.einsum('nk,nke->ne', topk_probs, onehot)
        h1 = jnp.einsum('nc,ehc->neh', flat, w1)
        h3 = jnp.einsum('nc,ehc->neh', flat, w3)
        h = jax.nn.silu(h1) * h3
        y = jnp.einsum('neh,ech->nec', h, w2)
        out = jnp.einsum('ne,nec->nc', gates, y)
        return out.reshape(B, T, C)
    x = x + _L0_gnn_ref(_layernorm(x, axis=-1), src, dst, L0_gnn_W1, L0_gnn_b1, L0_gnn_W2, L0_gnn_b2)
    x = x + _L0_ffn_ref(_layernorm(x, axis=-1)[None], L0_ffn_router_w, L0_ffn_w1, L0_ffn_w2, L0_ffn_w3)[0]
    return x

_drawn_inputs = setup_inputs


def setup_inputs(seed=0):
    import zlib

    import numpy as np

    out = dict(_drawn_inputs(seed))
    spreads = {'L0_gnn_b1': (0.0, 0.1), 'L0_gnn_b2': (0.0, 0.1)}
    factors = {}
    for name, (base, spread) in spreads.items():
        noise = np.random.default_rng([zlib.crc32(name.encode()), seed]).standard_normal(out[name].shape)
        drawn = base * np.exp(spread * noise) if base else spread * noise
        out[name] = jnp.asarray(drawn.astype(out[name].dtype))
    for name, factor in factors.items():
        out[name] = (out[name] * factor).astype(out[name].dtype)
    return out
```

```python
import concourse.bass as bass
from concourse import mybir
from contextlib import ExitStack

RMAX = bass.bass_isa.ReduceOp.max

P = 128
N, C, H, E = 6250, 256, 682, 8
GH = 512
NT = (N + P - 1) // P
ROWS = NT * P
DUMP = ROWS
ALLR = ROWS + P
EDGES = 106250
GT = 8
EG = (EDGES + P * GT - 1) // (P * GT)
ET = EG * GT
QT = 4
NCOPY = 4
TG = 7
NG = NT // TG
FT = (2 * ROWS + E * (P - 1)) // P
MT = FT + 3
TAB = (E - 1) * ROWS + MT * P
HC = 341
KC = 6
KH = 114
W13 = 2 * 4 * HC
W2C = KC * C
W2B = E * W13
WCOLS = W2B + E * W2C
WCH = WCOLS // EG
SY, SX, SW, SH = 64.0, 64.0, 64.0, 4.0
EPS = 1e-5

assert NT == TG * NG and WCH * EG == WCOLS and EG % 2 == 0 and FT % 2 == 1 and NG == 7


def gnn_moe(nc, x, srcT, dstT, src_rows, gw1t, gb1t, gw2, gb2, rwt, wall, out):
    f32, f16, bf16 = mybir.dt.float32, mybir.dt.float16, mybir.dt.bfloat16
    i32, u32 = mybir.dt.int32, mybir.dt.uint32
    ALU, ACT, AX = mybir.AluOpType, mybir.ActivationFunctionType, mybir.AxisListType
    ds = bass.ds
    Offset = bass.IndirectOffsetOnAxis

    dram = lambda name, shape, dt: nc.dram_tensor(name, shape, dt).ap()
    agg = [dram(f"agg{r}", (ALLR, C), f32) for r in range(NCOPY)]
    yhl = dram("yhl", (ALLR, 2 * C), f16)
    xhat_d = dram("xhat_d", (ALLR, C), f32)
    srow_d = dram("srow_d", (2, ET * P), f16)
    table = dram("table", (TAB, 2), i32)
    tiled = lambda t: t.rearrange("(t p) c -> p t c", p=P)
    x_t, out_t, yhl_t, xhat_t = tiled(x), tiled(out), tiled(yhl), tiled(xhat_d)
    agg_t = [tiled(a) for a in agg]

    with ExitStack() as ctx:
        sb = lambda name, shape, dt: ctx.enter_context(nc.sbuf_tensor(name, shape, dt))
        sem = lambda name: ctx.enter_context(nc.semaphore(name))

        WH = sb("WH", [P, WCOLS], f16)
        WL = sb("WL", [P, WCOLS], f16)
        WHf = WH[:, :].bitcast(f32)
        x_all = WHf[:, 0:NT * C].rearrange("p (t c) -> p t c", c=C)
        zeros = WHf[:, NT * C:NT * C + 2560]
        y_all = WL[:, 0:NT * 2 * C].rearrange("p (t c) -> p t c", c=2 * C)
        WLi = WL[:, :].bitcast(i32)
        T0 = NT * C
        tab_init = WLi[:, T0:T0 + 2 * (TAB // P)].rearrange("p (t w) -> p t w", w=2)
        T1 = T0 + 2 * (TAB // P)
        srow_i = WLi[:, T1:T1 + ET]
        srow_s = WLi[:, T1 + ET:T1 + 2 * ET]
        srow_h = WL[:, 2 * (T1 + 2 * ET):2 * (T1 + 2 * ET) + 2 * ET].rearrange("p (w t) -> p w t", w=2)
        assert 2 * (T1 + 2 * ET) + 2 * ET <= WCOLS and NT * C + 2560 <= WCOLS // 2

        iota_i = sb("iota_i", [P, P], i32)
        iota_f = sb("iota_f", [P, P], f32)
        iota_h = sb("iota_h", [P, P], f16)
        pcol_i = sb("pcol_i", [P, 1], i32)
        pcol = sb("pcol", [P, 1], f32)
        ident = sb("ident", [P, P], f32)
        before = sb("before", [P, P], f16)
        ones_h = sb("ones_h", [P, P], f16)
        ones_r = sb("ones_r", [1, P], f32)
        mix = sb("mix", [2, P], f16)
        pow_i = sb("pow_i", [P, 1], i32)
        pow_b = sb("pow_b", [P, 1], bf16)
        thr = sb("thr", [P, 1], f32)
        dumpcol = sb("dumpcol", [P, 1], f32)

        src_i = sb("src_i", [P, ET], i32)
        src_f = sb("src_f", [P, ET], f32)
        dst_i = sb("dst_i", [P, ET], i32)
        loc_f = sb("loc_f", [P, ET], f32)
        ext = sb("ext", [P, 2, EG], f32)
        exta = sb("exta", [P, 2, EG], f32)
        far = sb("far", [P, EG], f32)
        keep = sb("keep", [P, 2], f32)
        win_i = sb("win_i", [P, EG], i32)
        wide_f = sb("wide_f", [P, 1], f32)
        wide_i = sb("wide_i", [P, 1], i32)

        w12 = sb("w12", [P, 2, C], f32)
        b12 = sb("b12", [1, C], f32)
        b1col = sb("b1col", [P, 4], f32)
        b2row = sb("b2row", [1, C], f32)
        rw_sb = sb("rw_sb", [P, 2, E], f32)

        ROOM = 11520
        room = sb("room", [P, ROOM], f32)
        cur = [0]

        def take(words, dt, pattern=None, **sizes):
            v = room[:, cur[0]:cur[0] + words]
            cur[0] += words
            assert cur[0] <= ROOM, cur[0]
            if dt != f32:
                v = v.bitcast(dt)
            return v.rearrange(pattern, **sizes) if pattern else v

        ybuf = take(2 * GT * C, f16, "p (s k c) -> p s k c", s=2, k=GT)
        obuf = take(2 * GT * C, f32, "p (s k c) -> p s k c", s=2, k=GT)
        srow = take(GT * P, f16, "p (s n) -> p s n", s=2)
        wstage = take(2 * WCH, f32, "p (s n) -> p s n", s=2)
        eqb = take(QT * P, bf16, "p (q n) -> p q n", q=2)
        oneh = take(GT * P // 2, bf16, "p (k n) -> p k n", k=GT)
        msel = take(QT * P, f16, "p (q n) -> p q n", q=2)
        isdup = take(GT, f32)
        away = take(GT, f32)
        eidx = take(2 * GT, i32, "p (s k) -> p s k", s=2)
        gidx_b = take(1, i32)
        gw_a = room[:, 2 * GT * C:2 * GT * C + 8 * C].rearrange("p (j c) -> p j c", c=C)
        cur[0] = 0
        hsum = take(2 * TG * C, f32, "p (s t c) -> p s t c", s=2, t=TG)
        xres = take(2 * TG * C, f32, "p (s t c) -> p s t c", s=2, t=TG)
        xhat = take(TG * C, f32, "p (t c) -> p t c", t=TG)
        hT = take(2 * C, f32, "p (s k n) -> p s k n", s=2, k=2)
        xT = take(2 * C, f32, "p (s k n) -> p s k n", s=2, k=2)
        cur[0] = 0
        xg = take(2 * C, f32, "p (s c) -> p s c", s=2)
        xTh = take(C, f16, "p (s k n) -> p s k n", s=2, k=2)
        xTl = take(C, f16, "p (s k n) -> p s k n", s=2, k=2)
        sg = take(2 * HC, f32, "p (s n) -> p s n", s=2)
        hb = take(KC * KH, f32)
        hTh = take(KC * P // 2, f16, "p (j n) -> p j n", j=KC)
        hTl = take(KC * P // 2, f16, "p (j n) -> p j n", j=KC)
        yg = take(C, f32)
        slots = take(2 * MT, i32, "p (i w) -> p i w", w=2)
        slotsf = slots.bitcast(f32)

        bst = sb("bst", [P, TG, 6], f32)
        mv = sb("mv", [P, TG, 2], f32)
        rstd = sb("rstd", [P, TG], f32)
        mx = sb("mx", [P, TG, 8], f32)
        mxi = sb("mxi", [P, TG, 8], u32)
        sel = sb("sel", [P, 2, TG], f32)
        dif = sb("dif", [P, TG, 8], f32)
        exs = sb("exs", [P, TG, 8], f32)
        prb = sb("prb", [P, 4, TG], f32)
        oneh_e = sb("oneh_e", [P, 2, TG, E], f32)
        picked = sb("picked", [P, TG, E], f16)
        rank = sb("rank", [P, TG, E], f32)
        prod = sb("prod", [P, 2, TG, E], f32)
        place = sb("place", [P, 2, TG], f32)
        place_i = sb("place_i", [P, 2, TG], i32)
        base = sb("base", [P, E], f32)
        tok = sb("tok", [P, TG], f32)
        load_ = sb("load_", [P, TG, 2, 2], i32)
        loadf = load_[:, :, :, :].bitcast(f32)
        cnt = sb("cnt", [P, E], f32)
        cnt_i = sb("cnt_i", [P, E], i32)
        ntl = sb("ntl", [P, E], f32)
        tend = sb("tend", [P, E], f32)
        jump = sb("jump", [P, E], f32)
        tnum_i = sb("tnum_i", [P, MT], i32)
        tnum = sb("tnum", [P, MT], f32)
        past = sb("past", [P, MT], f32)
        acc_e = sb("acc_e", [P, MT], f32)
        acc_r = sb("acc_r", [P, MT], f32)
        meta = sb("meta", [P, 3, MT], i32)
        gidx = sb("gidx", [P, 2], i32)
        sidx = sb("sidx", [P, 1], i32)

        ps = ctx.enter_context(nc.psum_tensor("ps", [P, 8, 512], f32))

        s_in = sem("s_in")
        s_x = sem("s_x")
        s_gw = sem("s_gw")
        s_pool = sem("s_pool")
        s_zero = sem("s_zero")
        s_const = sem("s_const")
        s_dve = sem("s_dve")
        s_tab = sem("s_tab")
        s_srow = sem("s_srow")
        s_ext = sem("s_ext")
        s_ar = sem("s_ar")
        s_edges = sem("s_edges")
        s_w12 = sem("s_w12")
        s_w12c = sem("s_w12c")
        s_var = sem("s_var")
        s_sd = sem("s_sd")
        s_yn = sem("s_yn")
        s_yh = sem("s_yh")
        s_yl = sem("s_yl")
        s_init = sem("s_init")
        s_win = [sem(f"s_win{s}") for s in range(2)]
        s_row = [sem(f"s_row{s}") for s in range(2)]
        s_wst = [sem(f"s_wst{s}") for s in range(2)]
        s_bc = sem("s_bc")
        s_eq = sem("s_eq")
        s_one = sem("s_one")
        s_idx = sem("s_idx")
        s_sel = sem("s_sel")
        s_selc = sem("s_selc")
        s_o = sem("s_o")
        s_ob = sem("s_ob")
        s_wcp = sem("s_wcp")
        s_free = sem("s_free")
        s_add = [sem(f"s_add{r}") for r in range(NCOPY)]
        s_wh = sem("s_wh")
        s_wl = sem("s_wl")
        s_h0 = [sem(f"s_h0{s}") for s in range(2)]
        s_h3 = [sem(f"s_h3{s}") for s in range(2)]
        s_xr = [sem(f"s_xr{s}") for s in range(2)]
        s_ht = sem("s_ht")
        s_htc = sem("s_htc")
        s_z = sem("s_z")
        s_x2 = sem("s_x2")
        s_xn = sem("s_xn")
        s_xt = sem("s_xt")
        s_xtc = sem("s_xtc")
        s_lg = sem("s_lg")
        s_mx = sem("s_mx")
        s_ex = sem("s_ex")
        s_pk = sem("s_pk")
        s_rk = sem("s_rk")
        s_pos = sem("s_pos")
        s_scat = sem("s_scat")
        s_st = [sem(f"s_st{s}") for s in range(2)]
        s_sth = sem("s_sth")
        s_meta = sem("s_meta")
        s_slot = [sem(f"s_slot{s}") for s in range(2)]
        s_cp = sem("s_cp")
        s_xg = [sem(f"s_xg{s}") for s in range(2)]
        p_x = sem("p_x")
        a_x = sem("a_x")
        d_x = sem("d_x")
        p_h = sem("p_h")
        a_s = sem("a_s")
        d_h = sem("d_h")
        p_t = sem("p_t")
        a_t = sem("a_t")
        d_t = sem("d_t")
        p_y = sem("p_y")
        d_y = sem("d_y")
        s_acc = sem("s_acc")
        block = ctx.enter_context(nc.Block())

        ZW = 2560
        INIT_ALL = 16 * ((NCOPY - 1) * (ALLR // P * C // ZW) + 3 + 1 + 1 + 1 + 2 * NG)

        def part(v, i, n=1):
            return v[:, i:i + n] if isinstance(i, int) else v[:, ds(i, n)]

        def apart(eng):
            eng.nop(nofuse=True)

        def later(value):
            return not isinstance(value, int) or value > 0

        def turns(eng, body, count):
            body(0)
            with eng.Fori(1, count) as turn:
                body(turn)

        class Chain:

            def __init__(self, eng, s):
                self.eng, self.s, self.n, self.turn, self.start, self.steps = eng, s, 0, 0, 0, 0

            def __call__(self, ins):
                ins.then_inc(self.s, 1)
                self.n += 1
                self.eng.wait_ge(self.s, self.turn * self.steps + self.n)
                if self.steps:
                    apart(self.eng)

            def enter(self, turn, steps):
                if not self.steps:
                    self.start = self.n
                self.turn, self.steps, self.n = turn, steps, self.start

            def leave(self, count):
                assert self.n - self.start == self.steps, self.n - self.start
                self.n, self.turn, self.steps = self.start + count * self.steps, 0, 0

        @block.sync
        def _(sp):
            sp.dma_start(src_i[:, :], srcT).then_inc(s_in, 16)
            sp.dma_start(dst_i[:, :], dstT).then_inc(s_in, 16)
            sp.dma_start(srow_i, src_rows).then_inc(s_in, 16)
            for g in range(NG):
                t = slice(g * TG, (g + 1) * TG)
                sp.dma_start(x_all[:, t, :], x_t[:, t, :]).then_inc(s_x, 16)
            sp.dma_start(gw_a[:, 0:4, :], gw1t.rearrange("(j p) c -> p j c", p=P)).then_inc(s_gw, 16)
            sp.dma_start(gw_a[:, 4:8, :], gw2.rearrange("(j p) c -> p j c", p=P)).then_inc(s_gw, 16)
            sp.dma_start(b1col[:, :], gb1t).then_inc(s_gw, 16)
            sp.dma_start(b2row[:, :], gb2).then_inc(s_gw, 16)
            sp.dma_start(rw_sb[:, :, :], rwt.rearrange("(k p) e -> p k e", p=P)).then_inc(s_gw, 16)

            sp.wait_ge(s_zero, 1)
            for r in range(1, NCOPY):
                flat = agg[r].rearrange("(p t) c -> p (t c)", p=P)
                for k in range(ALLR // P * C // ZW):
                    sp.dma_start(flat[:, k * ZW:(k + 1) * ZW], zeros).then_inc(s_init, 16)
            for t in (agg[0], xhat_d, out):
                sp.dma_start(t[DUMP:ALLR, :], zeros[:, 0:C]).then_inc(s_init, 16)
            sp.dma_start(yhl[DUMP:ALLR, :], zeros[:, 0:C].bitcast(f16)).then_inc(s_init, 16)
            sp.wait_ge(s_tab, 1)
            sp.dma_start(table.rearrange("(p t) w -> p t w", p=P), tab_init).then_inc(s_init, 16)
            sp.wait_ge(s_srow, 1)
            sp.dma_start(srow_d.rearrange("w (p t) -> p w t", p=P), srow_h).then_inc(s_init, 16)
            for g in range(NG):
                t = slice(g * TG, (g + 1) * TG)
                sp.wait_ge(s_yl, g + 1)
                sp.dma_start(agg_t[0][:, t, :], x_all[:, t, :]).then_inc(s_init, 16)
                sp.dma_start(yhl_t[:, t, :], y_all[:, t, :]).then_inc(s_init, 16)

            sp.wait_ge(s_init, INIT_ALL)
            sp.wait_ge(s_edges, 1)
            wide = sp.value_load(wide_i[0:1, 0:1], min_val=0, max_val=1)

            def group_loads(g, s):
                win = sp.value_load(part(win_i[0:1, :], g), min_val=0, max_val=N - 1)
                sp.dma_start(srow[0:2, s, :], part(srow_d, g * GT * P, GT * P)).then_inc(s_row[s], 16)
                with sp.If(wide == 0):
                    for k in range(GT):
                        sp.dma_start(ybuf[16 * k:16 * k + 16, s, 0, :],
                                     yhl[ds(win + 16 * k, 16), :]).then_inc(s_win[s], 16)
                sp.dma_start(wstage[:, s, :], wall[g] if isinstance(g, int)
                             else wall[ds(g, 1), :, :].rearrange("a p n -> p (a n)")).then_inc(s_wst[s], 16)

            for g in range(2):
                group_loads(g, g)
            with sp.Fori(0, EG // 2 - 1) as it:
                for s in range(2):
                    g = it * 2 + s
                    sp.wait_ge(s_ob, g * 4 + 4)
                    apart(sp)
                    sp.wait_ge(s_wl, g + 1)
                    apart(sp)
                    group_loads(g + 2, s)

            for r in range(NCOPY):
                sp.wait_ge(s_add[r], 16 * (ET // NCOPY))
            sp.wait_ge(s_wl, EG)

            def sum_loads(g, s):
                a, b = (agg_t[0][:, g * TG:(g + 1) * TG], x_t[:, g * TG:(g + 1) * TG]) if isinstance(g, int) \
                    else (agg_t[0][:, ds(g * TG, TG)], x_t[:, ds(g * TG, TG)])
                sp.dma_start(hsum[:, s, :, :], a).then_inc(s_h0[s], 16)
                sp.dma_start(xres[:, s, :, :], b).then_inc(s_xr[s], 16)

            def sum_loads_behind(g, s, turn):
                sp.wait_ge(s_ht, g * TG + TG)
                apart(sp)
                sp.wait_ge(s_xn, g * TG + TG)
                apart(sp)
                sp.wait_ge(s_st[s], turn * 16 + 16)
                apart(sp)
                sum_loads(g + 2, s)

            sum_loads(0, 0)
            sum_loads(1, 1)
            with sp.Fori(0, 2) as it:
                for s in range(2):
                    sum_loads_behind(it * 2 + s, s, it)
            sum_loads_behind(4, 0, 2)

            sp.wait_ge(s_meta, 1)
            sp.wait_ge(s_scat, 16 * 2 * NT)
            for s in range(2):
                sp.wait_ge(s_st[s], 16 * ((NG + 1 - s) // 2))
            sp.wait_ge(s_sth, 16 * NG)
            def slot_loads(it):
                for s in range(2):
                    i = it * 2 + s
                    row = sp.value_load(meta[0:1, 0, ds(i, 1)], min_val=0, max_val=TAB - P)
                    if later(it * 16):
                        sp.wait_ge(s_slot[s], it * 16)
                    apart(sp)
                    sp.dma_start(slots[:, ds(i, 1), :],
                                 table[ds(row, P), :].rearrange("(a p) w -> p a w", p=P)).then_inc(s_slot[s], 16)

            turns(sp, slot_loads, MT // 2)
            for s in range(2):
                sp.wait_ge(s_slot[s], MT // 2 * 16)
        @block.gpsimd
        def _(pool):
            chain = Chain(pool, s_pool)
            chain(pool.memset(zeros, 0.0))
            chain(pool.iota(tab_init, pattern=[[1, TAB // P], [0, 2]], base=0, channel_multiplier=TAB // P))
            chain(pool.memset(tab_init[:, :, 1:2], 0))
            pool.sem_inc(s_zero, 1)
            chain(pool.iota(iota_i[:, :], pattern=[[1, P]], base=0, channel_multiplier=0))
            chain(pool.iota(pcol_i[:, :], pattern=[[0, 1]], base=0, channel_multiplier=1))
            chain(pool.iota(tnum_i[:, :], pattern=[[1, MT]], base=0, channel_multiplier=0))
            chain(pool.iota(pow_i[:, :], pattern=[[0, 1]], base=127 + 63, channel_multiplier=-1))
            chain(pool.memset(ident[:, :], 0.0))
            chain(pool.affine_select(out=ident[:, :], in_=ident[:, :], compare_op=ALU.not_equal, fill=1.0,
                                     base=0, pattern=[[-1, P]], channel_multiplier=1))
            chain(pool.memset(ones_h[:, :], 1.0))
            chain(pool.affine_select(out=before[:, :], in_=ones_h[:, :], compare_op=ALU.is_gt, fill=0.0,
                                     base=0, pattern=[[1, P]], channel_multiplier=-1))
            chain(pool.memset(ones_r[:, :], 1.0))
            chain(pool.memset(mix[:, :], 1.0))
            chain(pool.memset(mix[0:1, :], 64.0))
            pool.sem_inc(s_const, 1)
            pool.wait_ge(s_ext, 1)
            pool.partition_all_reduce(exta[:, :, :].rearrange("p a g -> p (a g)"),
                                      ext[:, :, :].rearrange("p a g -> p (a g)"), P, RMAX).then_inc(s_ar, 1)

            pool.wait_ge(s_init, INIT_ALL)
            pool.wait_ge(s_edges, 1)
            wide = pool.value_load(wide_i[0:1, 0:1], min_val=0, max_val=1)
            def edge_groups(it):
                for s in range(2):
                    g = it * 2 + s
                    with pool.If(wide == 1):
                        if later(g * 4):
                            pool.wait_ge(s_ob, g * 4)
                        for k in range(GT):
                            if later((it * GT + k) * 16):
                                pool.wait_ge(s_win[s], (it * GT + k) * 16)
                            pool.tensor_copy(gidx_b, dst_i[:, ds(g * GT + k, 1)]).then_inc(s_wcp, 1)
                            pool.wait_ge(s_wcp, g * GT + k + 1)
                            apart(pool)
                            pool.indirect_dma_start(ybuf[:, s, k, :], None, yhl[:, :],
                                                    Offset(ap=gidx_b, axis=0)).then_inc(s_win[s], 16)
                        pool.wait_ge(s_win[s], (it + 1) * GT * 16)
                    pool.wait_ge(s_idx, g + 1)
                    for k in range(GT):
                        if k % 2 == 0:
                            pool.wait_ge(s_ob, g * 4 + k // 2 + 1)
                        r = k % NCOPY
                        if later((g * (GT // NCOPY) + k // NCOPY) * 16):
                            pool.wait_ge(s_add[r], (g * (GT // NCOPY) + k // NCOPY) * 16)
                        apart(pool)
                        pool.indirect_dma_start(agg[r][:, :], Offset(ap=eidx[:, s, k:k + 1], axis=0),
                                                obuf[:, s, k, :], None, bounds_check=ALLR - 1, oob_is_err=True,
                                                compute_op=ALU.add).then_inc(s_add[r], 16)
                        if k == NCOPY - 1:
                            pool.sem_inc(s_free, 1)

            turns(pool, edge_groups, EG // 2)
            for r in range(NCOPY):
                pool.wait_ge(s_add[r], 16 * (ET // NCOPY))

            def add_copy(g, s, turn, r):
                if r == 1:
                    pool.wait_ge(s_h0[s], turn * 16 + 16)
                else:
                    pool.wait_ge(s_h3[s], turn * (16 * (NCOPY - 1)) + 16 * (r - 1))
                apart(pool)
                a = agg_t[r][:, g * TG:(g + 1) * TG] if isinstance(g, int) else agg_t[r][:, ds(g * TG, TG)]
                pool.dma_start(hsum[:, s, :, :], a, accum_op=ALU.add).then_inc(s_h3[s], 16)

            def scatter_group(g, adds):
                pool.wait_ge(s_pos, g + 1)
                apart(pool)
                for t in range(TG):
                    for k in range(2):
                        pool.indirect_dma_start(table[:, :], Offset(ap=place_i[:, k, t:t + 1], axis=0),
                                                load_[:, t, k, :], None).then_inc(s_scat, 16)
                    if adds and t in (1, 3, 5):
                        add_copy(*adds, 1 + (t - 1) // 2)

            for g in range(2):
                for r in range(1, NCOPY):
                    add_copy(g, g, 0, r)
            with pool.Fori(0, 2) as it:
                for s in range(2):
                    scatter_group(it * 2 + s, (it * 2 + s + 2, s, it + 1))
            scatter_group(4, (6, 0, 3))
            scatter_group(5, None)
            scatter_group(6, None)

            def fetch(i, s, seen, done, copies):
                pool.wait_ge(s_slot[s], seen)
                if later(done):
                    pool.wait_ge(p_x, done)
                pool.tensor_copy(gidx[:, s:s + 1], slots[:, i, 0:1] if isinstance(i, int)
                                 else slots[:, ds(i, 1), 0]).then_inc(s_cp, 1)
                pool.wait_ge(s_cp, copies)
                apart(pool)
                pool.indirect_dma_start(xg[:, s, :], None, xhat_d[:, :],
                                        Offset(ap=gidx[:, s:s + 1], axis=0)).then_inc(s_xg[s], 16)

            def add_out(i, copies):
                if later(i * 16):
                    pool.wait_ge(s_acc, i * 16)
                pool.tensor_copy(sidx[:, :], slots[:, i, 0:1] if isinstance(i, int)
                                 else slots[:, ds(i, 1), 0]).then_inc(s_cp, 1)
                pool.wait_ge(s_cp, copies)
                pool.wait_ge(d_y, i + 1)
                apart(pool)
                pool.indirect_dma_start(out[:, :], Offset(ap=sidx[:, :], axis=0), yg, None,
                                        bounds_check=ALLR - 1, oob_is_err=True,
                                        compute_op=ALU.add).then_inc(s_acc, 16)

            pool.wait_ge(s_sth, 16 * NG)
            for s in range(2):
                pool.wait_ge(s_st[s], 16 * ((NG + 1 - s) // 2))
            for i in range(3):
                fetch(i, i % 2, i // 2 * 16 + 16, i - 1, i + 1)

            def tiles(it):
                for o in range(2):
                    i = it * 2 + 1 + o
                    fetch(i + 2, 1 - o, it * 16 + 32 + 16 * o, i + 1, it * 4 + 2 * o + 4)
                    add_out(i - 1, it * 4 + 2 * o + 5)

            turns(pool, tiles, FT // 2)
            add_out(FT - 1, 2 * FT + 2)
            pool.wait_ge(s_acc, 16 * FT)
            pool.wait_ge(s_xg[0], 16 * (FT // 2 + 2))
            pool.wait_ge(s_xg[1], 16 * (FT // 2 + 1))

        @block.tensor
        def _(pe):
            mm = nc.tensor.matmul

            pe.wait_ge(s_gw, 80)
            pe.wait_ge(s_const, 1)
            for k in range(2):
                for j in range(4):
                    mm(ps[:, k, 0:C], gw_a[:, j, k * P:(k + 1) * P], gw_a[:, 4 + j, :], start=j == 0, stop=j == 3)
            for j in range(4):
                mm(ps[0:1, 2, 0:C], b1col[:, j:j + 1], gw_a[:, 4 + j, :], start=j == 0, stop=False)
            mm(ps[0:1, 2, 0:C], ones_r[0:1, 0:1], b2row[:, :], start=False, stop=True).then_inc(s_w12, 1)
            pe.wait_ge(s_w12c, 1)

            pe.wait_ge(s_edges, 1)
            wide = pe.value_load(wide_i[0:1, 0:1], min_val=0, max_val=1)
            def edge_groups(it):
                for s in range(2):
                    g = it * 2 + s
                    pe.wait_ge(s_row[s], it * 16 + 16)
                    if later(g * 2):
                        pe.wait_ge(s_eq, g * 2)
                    for q in range(2):
                        mm(ps[:, q, :], mix[:, :], srow[0:2, s, q * QT * P:(q + 1) * QT * P],
                           start=True, stop=True).then_inc(s_bc, 1)
                    pe.wait_ge(s_one, g + 1)
                    if later(g):
                        pe.wait_ge(s_idx, g)
                    for q in range(2):
                        pe.wait_ge(s_eq, g * 2 + q + 1)
                        for k in range(QT):
                            e = eqb[:, q, k * P:(k + 1) * P]
                            mm(ps[:, 6, q * QT + k:q * QT + k + 1], e, pow_b[:, :], start=True, stop=True)
                        for k in range(QT):
                            e = eqb[:, q, k * P:(k + 1) * P]
                            last = mm(ps[:, 2 + q, k * P:(k + 1) * P], oneh[:, q * QT + k, :], e,
                                      start=True, stop=True)
                        last.then_inc(s_sel, 1)
                    pe.wait_ge(s_win[s], it * (16 * GT) + 16 * GT)
                    for j in range(GT // 2):
                        if j % 2 == 0:
                            pe.wait_ge(s_selc, g * 2 + j // 2 + 1)
                        if j >= 2:
                            pe.wait_ge(s_ob, g * 4 + j - 1)
                        for k in (2 * j, 2 * j + 1):
                            rows = ybuf[:, s, 0, :] if k == 0 else ybuf[:, s, ds(wide * k, 1), :]
                            m = msel[:, k // QT, (k % QT) * P:(k % QT + 1) * P]
                            for h in range(2):
                                y = rows[:, h * C:(h + 1) * C] if k == 0 else \
                                    rows[:, :, h * C:(h + 1) * C].rearrange("p a c -> p (a c)")
                                last = mm(ps[:, 4 + j % 2, (k % 2) * C:(k % 2 + 1) * C], m, y,
                                          start=h == 0, stop=h == 1)
                        last.then_inc(s_o, 1)

            turns(pe, edge_groups, EG // 2)
            def node_group(g, s, turn):
                pe.wait_ge(s_h3[s], turn * (16 * (NCOPY - 1)) + 16 * (NCOPY - 1))
                if later(g * TG):
                    pe.wait_ge(s_htc, g * TG)
                if later(g * TG):
                    pe.wait_ge(s_x2, g * TG)

                def turn_sum(t):
                    if t >= 2:
                        pe.wait_ge(s_htc, g * TG + t - 1)
                    for k in range(2):
                        last = nc.tensor.transpose(ps[:, t % 2, k * P:(k + 1) * P],
                                                   hsum[:, s, t, k * P:(k + 1) * P], ident[:, :])
                    last.then_inc(s_ht, 1)

                turn_sum(0)
                for t in range(TG):
                    if t + 1 < TG:
                        turn_sum(t + 1)
                    if t >= 2:
                        pe.wait_ge(s_x2, g * TG + t - 1)
                    pe.wait_ge(s_htc, g * TG + t + 1)
                    z = ps[:, 2 + t % 2, 0:C]
                    for k in range(2):
                        mm(z, hT[:, t % 2, k, :], w12[:, k, :], start=k == 0, stop=False)
                    mm(z, ones_r[:, :], b12[:, :], start=False, stop=True).then_inc(s_z, 1)

                def turn_x(t):
                    if t >= 2:
                        pe.wait_ge(s_xtc, g * TG + t - 1)
                    pe.wait_ge(s_xn, g * TG + t + 1)
                    for k in range(2):
                        last = nc.tensor.transpose(ps[:, 4 + t % 2, k * P:(k + 1) * P],
                                                   xhat[:, t, k * P:(k + 1) * P], ident[:, :])
                    last.then_inc(s_xt, 1)

                if later(g * TG):
                    pe.wait_ge(s_xtc, g * TG)
                if later(g):
                    pe.wait_ge(s_mx, g)
                turn_x(0)
                for t in range(TG):
                    if t + 1 < TG:
                        turn_x(t + 1)
                    pe.wait_ge(s_xtc, g * TG + t + 1)
                    for k in range(2):
                        last = mm(ps[:, 6, t * E:(t + 1) * E], xT[:, t % 2, k, :], rw_sb[:, k, :],
                                  start=k == 0, stop=k == 1)
                    last.then_inc(s_lg, 1)

                pe.wait_ge(s_pk, g + 1)
                if later(g):
                    pe.wait_ge(s_pos, g)
                flat = picked[:, :, :].rearrange("p t e -> p (t e)")
                mm(ps[:, 7, 0:TG * E], before[:, :], flat, start=True, stop=False, skip_group_check=True)
                for d in range(1, TG):
                    mm(ps[:, 7, d * E:TG * E], ones_h[:, :], flat[:, 0:(TG - d) * E], start=False,
                       stop=d == TG - 1, skip_group_check=True)
                for t in range(TG):
                    last = mm(ps[:, 7, 64:64 + E], ones_h[:, :], picked[:, t, :], start=t == 0, stop=t == TG - 1)
                last.then_inc(s_rk, 1)

            def node_groups(it):
                for s in range(2):
                    node_group(it * 2 + s, s, it)

            turns(pe, node_groups, 3)
            node_group(6, 0, 3)

            def turn_tile(i, s, seen):
                pe.wait_ge(s_xg[s], seen)
                if later(i):
                    pe.wait_ge(d_x, i)
                for k in range(2):
                    last = nc.tensor.transpose(ps[:, 6, k * P:(k + 1) * P], xg[:, s, k * P:(k + 1) * P], ident[:, :])
                last.then_inc(p_x, 1)

            def hidden(i, s, halves, col, first):
                for c in halves:
                    if not first:
                        pe.wait_ge(d_h, i * 2 - 1 + c)
                    for k, (xp, wp) in enumerate(((xTh, WH), (xTh, WL), (xTl, WH))):
                        for kk in range(2):
                            for m in range(2):
                                o = kk * 4 * HC + c * 2 * HC + m * HC
                                last = mm(ps[:, 2 * c + m, 0:HC], xp[:, s, kk, :], wp[:, ds(col + o, HC)],
                                          start=k == 0 and kk == 0, stop=k == 2 and kk == 1)
                    last.then_inc(p_h, 1)

            def turn_h(i):
                pe.wait_ge(d_h, i * 2 + 2)
                if later(i * 2):
                    pe.wait_ge(d_t, i * 2)
                for j in range(KC):
                    last = nc.tensor.transpose(ps[0:KH, 4 + j // 3, (j % 3) * P:(j % 3 + 1) * P],
                                               hb[:, j * KH:(j + 1) * KH], ident[:, :])
                    if j % 3 == 2:
                        last.then_inc(p_t, 1)

            def output(i, col):
                pe.wait_ge(d_t, i * 2 + 2)
                if later(i):
                    pe.wait_ge(d_y, i)
                for j in range(KC):
                    for n, (hp, wp) in enumerate(((hTh, WH), (hTh, WL), (hTl, WH))):
                        last = mm(ps[:, 7, 0:C], hp[0:KH, j, :], wp[0:KH, ds(col + j * C, C)],
                                  start=j == 0 and n == 0, stop=j == KC - 1 and n == 2)
                last.then_inc(p_y, 1)

            def column(row, i):
                v = meta[0:1, row, i:i + 1] if isinstance(i, int) else meta[0:1, row, ds(i, 1)]
                return pe.value_load(v, min_val=0 if row == 1 else W2B,
                                     max_val=(E - 1) * W13 if row == 1 else W2B + (E - 1) * W2C)

            pe.wait_ge(s_meta, 1)
            turn_tile(0, 0, 16)
            pe.wait_ge(d_x, 1)
            hidden(0, 0, (0,), column(1, 0), True)
            turn_tile(1, 1, 16)
            hidden(0, 0, (1,), column(1, 0), True)
            def tiles(it):
                for o in range(2):
                    i = it * 2 + 1 + o
                    w13, w2 = column(1, i), column(2, i - 1)
                    turn_h(i - 1)
                    pe.wait_ge(d_x, i + 1)
                    hidden(i, 1 - o, (0,), w13, False)
                    turn_tile(i + 1, o, it * 16 + 32)
                    hidden(i, 1 - o, (1,), w13, False)
                    output(i - 1, w2)

            turns(pe, tiles, FT // 2)
            turn_h(FT - 1)
            output(FT - 1, column(2, FT - 1))

        @block.scalar
        def _(act):
            copy = lambda o, i, scale=1.0: nc.scalar.activation(o, i, ACT.Copy, scale=scale)
            act.wait_ge(s_w12, 1)
            copy(w12[:, :, :], ps[:, 0:2, 0:C])
            copy(b12[:, :], ps[0:1, 2, 0:C]).then_inc(s_w12c, 1)

            def roots(n):
                act.wait_ge(s_var, n)
                nc.scalar.activation(rstd[:, :], mv[:, :, 1], ACT.Sqrt).then_inc(s_sd, 1)

            with act.Fori(0, NG) as g:
                roots(g + 1)
                act.wait_ge(s_yn, g + 1)
                copy(y_all[:, ds(g * TG, TG), 0:C], x_all[:, ds(g * TG, TG), :], SY).then_inc(s_yh, 1)

            act.wait_ge(s_init, INIT_ALL)
            def edge_groups(it):
                for s in range(2):
                    g = it * 2 + s
                    for q in range(2):
                        act.wait_ge(s_sel, g * 2 + q + 1)
                        copy(msel[:, q, :], ps[:, 2 + q, :]).then_inc(s_selc, 1)
                    if later(g):
                        act.wait_ge(s_free, g)
                    for j in range(GT // 2):
                        act.wait_ge(s_o, g * 4 + j + 1)
                        copy(obuf[:, s, 2 * j:2 * j + 2, :], ps[:, 4 + j % 2, :].rearrange("p (k c) -> p k c", k=2),
                             1.0 / SY).then_inc(s_ob, 1)
                    act.wait_ge(s_wst[s], it * 16 + 16)
                    copy(WH[:, ds(g * WCH, WCH)], wstage[:, s, :], SW).then_inc(s_wh, 1)

            turns(act, edge_groups, EG // 2)
            def node_group(g, s):
                for t in range(TG):
                    act.wait_ge(s_ht, g * TG + t + 1)
                    if later(g * TG + (t - 1 if t >= 2 else 0)):
                        act.wait_ge(s_z, g * TG + (t - 1 if t >= 2 else 0))
                    copy(hT[:, t % 2, :, :], ps[:, t % 2, 0:C].rearrange("p (k n) -> p k n", k=2)).then_inc(s_htc, 1)
                act.wait_ge(s_x2, g * TG + TG)
                o = out_t[:, g * TG:(g + 1) * TG] if isinstance(g, int) else out_t[:, ds(g * TG, TG)]
                act.dma_start(o, xres[:, s, :, :]).then_inc(s_st[s], 16)
                roots(g + NG + 1)
                for t in range(TG):
                    act.wait_ge(s_xt, g * TG + t + 1)
                    if later(g * TG + (t - 1 if t >= 2 else 0)):
                        act.wait_ge(s_lg, g * TG + (t - 1 if t >= 2 else 0))
                    copy(xT[:, t % 2, :, :], ps[:, 4 + t % 2, 0:C].rearrange("p (k n) -> p k n", k=2)).then_inc(s_xtc, 1)
                o = xhat_t[:, g * TG:(g + 1) * TG] if isinstance(g, int) else xhat_t[:, ds(g * TG, TG)]
                act.dma_start(o, xhat).then_inc(s_sth, 16)
                act.wait_ge(s_mx, g + 1)
                nc.scalar.activation(exs[:, :, :], dif[:, :, :], ACT.Exp).then_inc(s_ex, 1)

            def node_groups(it):
                for s in range(2):
                    node_group(it * 2 + s, s)

            turns(act, node_groups, 3)
            node_group(6, 0)

            def high_x(i, s):
                act.wait_ge(p_x, i + 1)
                if not isinstance(i, int) or i > 1:
                    act.wait_ge(p_h, i * 2 - 2)
                copy(xTh[:, s, :, :], ps[:, 6, 0:C].rearrange("p (k n) -> p k n", k=2), SX).then_inc(a_x, 1)

            def high_h(i):
                for c in range(2):
                    act.wait_ge(p_t, i * 2 + c + 1)
                    if c == 0:
                        if later(i):
                            act.wait_ge(p_y, i)
                    copy(hTh[0:KH, 3 * c:3 * c + 3, :],
                         ps[0:KH, 4 + c, 0:3 * P].rearrange("p (j n) -> p j n", j=3)).then_inc(a_t, 1)

            def silu(i, c, first=False):
                act.wait_ge(p_h, i * 2 + c + 1)
                if not first:
                    act.wait_ge(d_h, i * 2 - 1 + c)
                nc.scalar.activation(sg[:, c, :], ps[:, 2 * c, 0:HC], ACT.Silu,
                                     scale=1.0 / (SX * SW)).then_inc(a_s, 1)

            high_x(0, 0)
            silu(0, 0, True)
            high_x(1, 1)
            silu(0, 1, True)
            def tiles(it):
                for o in range(2):
                    i = it * 2 + 1 + o
                    high_h(i - 1)
                    silu(i, 0)
                    high_x(i + 1, o)
                    silu(i, 1)

            turns(act, tiles, FT // 2)
            high_h(FT - 1)

        @block.vector
        def _(dve):
            v = nc.vector
            chain = Chain(dve, s_dve)
            cp = v.tensor_copy
            dve.wait_ge(s_zero, 1)
            t0 = tab_init[:, :, 0]
            chain(v.tensor_scalar(t0, t0, P - 1, None, ALU.bitwise_and))
            v.tensor_scalar(t0, t0, DUMP, None, ALU.add).then_inc(s_tab, 1)
            dve.wait_ge(s_in, 48)
            chain(v.tensor_scalar(srow_s, srow_i, 6, None, ALU.logical_shift_right))
            chain(cp(srow_h[:, 0, :], srow_s))
            chain(v.tensor_scalar(srow_s, srow_i, 63, None, ALU.bitwise_and))
            cp(srow_h[:, 1, :], srow_s).then_inc(s_srow, 1)
            chain(cp(loc_f[:, :], dst_i[:, :]))
            grouped = loc_f[:, :].rearrange("p (g k) -> p g k", k=GT)
            v.tensor_reduce(ext[:, 0, :], grouped, AX.X, ALU.max)
            chain(v.tensor_reduce(ext[:, 1, :], grouped, AX.X, ALU.min))
            v.tensor_scalar(ext[:, 1, :], ext[:, 1, :], -1.0, None, ALU.mult).then_inc(s_ext, 1)
            dve.wait_ge(s_const, 1)
            cp(iota_f[:, :], iota_i[:, :])
            cp(iota_h[:, :], iota_i[:, :])
            cp(pcol[:, :], pcol_i[:, :])
            cp(tnum[:, :], tnum_i[:, :])
            chain(v.tensor_scalar(pow_i[:, :], pow_i[:, :], 23, None, ALU.logical_shift_left))
            cp(pow_b[:, :], pow_i[:, :].bitcast(f32))
            v.tensor_scalar(thr[:, :], pow_i[:, :].bitcast(f32), 2.5, None, ALU.mult)
            v.tensor_scalar(dumpcol[:, :], pcol[:, :], float(DUMP), None, ALU.add)
            v.tensor_scalar(base[:, :], iota_f[:, 0:E], float(ROWS), None, ALU.mult)
            v.tensor_scalar(tok[:, :], iota_f[:, 0:TG], float(P), None, ALU.mult)
            chain(cp(src_f[:, :], src_i[:, :]))
            chain(v.tensor_scalar(tok[:, :], tok[:, :], pcol[:, 0:1], None, ALU.add))
            dve.wait_ge(s_ar, 1)
            v.tensor_scalar(win_i[:, :], exta[:, 1, :], -1.0, None, ALU.mult)
            chain(v.tensor_tensor(far[:, :], exta[:, 0, :], exta[:, 1, :], ALU.add))
            chain(v.tensor_reduce(keep[:, 0:1], far[:, :], AX.X, ALU.max))
            chain(v.tensor_scalar(wide_f[:, :], keep[:, 0:1], float(P), None, ALU.is_ge))
            cp(wide_i[:, :], wide_f[:, :])
            v.tensor_tensor(grouped, grouped, exta[:, 1, :].unsqueeze(2).broadcast_to([P, EG, GT]), ALU.add)
            v.tensor_scalar(keep[:, 0:1], wide_f[:, :], -1.0, 1.0, ALU.mult, ALU.add)
            chain(v.tensor_tensor(keep[:, 1:2], wide_f[:, :], pcol[:, :], ALU.mult))
            v.tensor_scalar(loc_f[:, :], loc_f[:, :], keep[:, 0:1], keep[:, 1:2], ALU.mult, ALU.add)\
                .then_inc(s_edges, 1)

            def norms(src, n):
                for t in range(TG):
                    last = v.bn_stats(bst[:, t, :], src(t))
                chain(last)
                for t in range(TG):
                    last = v.bn_aggr(mv[:, t, :], bst[:, t, :])
                chain(last)
                v.tensor_scalar(mv[:, :, 1], mv[:, :, 1], EPS, None, ALU.add).then_inc(s_var, 1)
                dve.wait_ge(s_sd, n)
                chain(v.reciprocal(rstd[:, :], rstd[:, :]))

            def normed(out_, in_, t):
                return v.tensor_scalar(out_, in_, mv[:, t, 0:1], rstd[:, t:t + 1], ALU.subtract, ALU.mult)

            dve.wait_ge(s_x, 16 * NG)
            with dve.Fori(0, NG) as g:
                chain.enter(g, 3)
                tile = lambda t: x_all[:, ds(g * TG + t, 1), :].rearrange("p a c -> p (a c)")
                norms(tile, g + 1)
                for t in range(TG):
                    last = normed(tile(t), tile(t), t)
                last.then_inc(s_yn, 1)
                dve.wait_ge(s_yh, g + 1)
                v.scalar_tensor_tensor(y_all[:, ds(g * TG, TG), C:2 * C], x_all[:, ds(g * TG, TG), :], SY,
                                       y_all[:, ds(g * TG, TG), 0:C], ALU.mult, ALU.subtract).then_inc(s_yl, 1)
                chain.leave(NG)

            dve.wait_ge(s_init, INIT_ALL)
            def edge_groups(it):
                chain.enter(it, 2 * 3)
                for s in range(2):
                    g = it * 2 + s
                    if later(g * 2):
                        dve.wait_ge(s_sel, g * 2)
                    v.tensor_tensor(oneh, iota_h[:, :].unsqueeze(1).broadcast_to([P, GT, P]),
                                    loc_f[:, ds(g * GT, GT)].unsqueeze(2).broadcast_to([P, GT, P]),
                                    ALU.is_equal).then_inc(s_one, 1)
                    for q in range(2):
                        dve.wait_ge(s_bc, g * 2 + q + 1)
                        v.tensor_tensor(eqb[:, q, :].rearrange("p (k n) -> p k n", k=QT),
                                        ps[:, q, :].rearrange("p (k n) -> p k n", k=QT),
                                        src_f[:, ds(g * GT + q * QT, QT)].unsqueeze(2).broadcast_to([P, QT, P]),
                                        ALU.is_equal).then_inc(s_eq, 1)
                    if later(g):
                        dve.wait_ge(s_wh, g)
                    dve.wait_ge(s_sel, g * 2 + 2)
                    if later(g):
                        dve.wait_ge(s_free, g)
                    v.tensor_scalar(isdup, ps[:, 6, 0:GT], thr[:, 0:1], None, ALU.is_gt)
                    chain(v.tensor_scalar(away, src_f[:, ds(g * GT, GT)], -1.0, dumpcol[:, 0:1], ALU.mult, ALU.add))
                    chain(v.tensor_tensor(away, away, isdup, ALU.mult))
                    chain(v.tensor_tensor(away, away, src_f[:, ds(g * GT, GT)], ALU.add))
                    cp(eidx[:, s, :], away).then_inc(s_idx, 1)
                    dve.wait_ge(s_wh, g + 1)
                    v.scalar_tensor_tensor(WL[:, ds(g * WCH, WCH)], wstage[:, s, :], SW, WH[:, ds(g * WCH, WCH)],
                                           ALU.mult, ALU.subtract).then_inc(s_wl, 1)

            turns(dve, edge_groups, EG // 2)
            chain.leave(EG // 2)
            def over(col):
                return col.unsqueeze(2).broadcast_to([P, TG, E])

            def node_group(g, s, turn):
                dve.wait_ge(s_xr[s], turn * 16 + 16)
                for t in range(TG):
                    dve.wait_ge(s_z, g * TG + t + 1)
                    v.tensor_tensor(xres[:, s, t, :], ps[:, 2 + t % 2, 0:C], xres[:, s, t, :],
                                    ALU.add).then_inc(s_x2, 1)
                dve.wait_ge(s_x2, g * TG + TG)
                norms(lambda t: xres[:, s, t, :], g + NG + 1)
                if later(g * 16):
                    dve.wait_ge(s_sth, g * 16)
                if later(g * TG):
                    dve.wait_ge(s_xt, g * TG)
                for t in range(TG):
                    normed(xhat[:, t, :], xres[:, s, t, :], t).then_inc(s_xn, 1)
                dve.wait_ge(s_lg, g * TG + TG)
                apart(dve)
                logits = lambda t: ps[:, 6, t * E:(t + 1) * E]
                for t in range(TG):
                    last = v.max(mx[:, t, :], logits(t))
                chain(last)
                for t in range(TG):
                    last = v.max_index(mxi[:, t, :], mx[:, t, :], logits(t))
                chain(last)
                v.tensor_tensor(dif[:, :, :], mx[:, :, :], over(mx[:, :, 0]), ALU.subtract).then_inc(s_mx, 1)
                chain(cp(sel[:, :, :], mxi[:, :, 0:2].rearrange("p t k -> p k t")))
                for k in range(2):
                    last = v.tensor_tensor(oneh_e[:, k, :, :], iota_f[:, 0:E].unsqueeze(1).broadcast_to([P, TG, E]),
                                           over(sel[:, k, :]), ALU.is_equal)
                chain(last)
                v.tensor_tensor(picked[:, :, :], oneh_e[:, 0, :, :], oneh_e[:, 1, :, :], ALU.add).then_inc(s_pk, 1)
                dve.wait_ge(s_ex, g + 1)
                chain(v.tensor_reduce(prb[:, 0, :], exs[:, :, :], AX.X, ALU.add))
                chain(v.reciprocal(prb[:, 1, :], prb[:, 0, :]))
                chain(v.tensor_tensor(prb[:, 2, :], exs[:, :, 1], prb[:, 1, :], ALU.mult))
                chain(v.tensor_tensor(prb[:, 1, :], exs[:, :, 0], prb[:, 1, :], ALU.mult))
                chain(v.tensor_tensor(prb[:, 3, :], prb[:, 1, :], prb[:, 2, :], ALU.add))
                chain(v.tensor_scalar(prb[:, 3, :], prb[:, 3, :], 1e-9, None, ALU.add))
                chain(v.reciprocal(prb[:, 0, :], prb[:, 3, :]))
                if later(g * (16 * 2 * TG)):
                    dve.wait_ge(s_scat, g * (16 * 2 * TG))
                for k in range(2):
                    v.tensor_tensor(loadf[:, :, k, 1], prb[:, 1 + k, :], prb[:, 0, :], ALU.mult)
                    last = cp(load_[:, :, k, 0], tok[:, :])
                chain(last)
                chain(v.tensor_scalar(tok[:, :], tok[:, :], float(TG * P), None, ALU.add))
                dve.wait_ge(s_rk, g + 1)
                chain(v.tensor_tensor(rank[:, :, :], ps[:, 7, 0:TG * E].rearrange("p (t e) -> p t e", e=E),
                                      base[:, :].unsqueeze(1).broadcast_to([P, TG, E]), ALU.add))
                v.tensor_tensor(base[:, :], ps[:, 7, 64:64 + E], base[:, :], ALU.add)
                for k in range(2):
                    last = v.tensor_tensor(prod[:, k, :, :], oneh_e[:, k, :, :], rank[:, :, :], ALU.mult)
                chain(last)
                for k in range(2):
                    last = v.tensor_reduce(place[:, k, :], prod[:, k, :, :], AX.X, ALU.add)
                chain(last)
                cp(place_i[:, :, :], place[:, :, :]).then_inc(s_pos, 1)

            CS = 19
            def node_groups(it):
                chain.enter(it, 2 * CS)
                for s in range(2):
                    node_group(it * 2 + s, s, it)

            turns(dve, node_groups, 3)
            chain.leave(3)
            node_group(6, 0, 3)

            dve.wait_ge(s_pos, NG)
            chain(v.tensor_scalar(cnt[:, :], iota_f[:, 0:E], -float(ROWS), float(P - 1), ALU.mult, ALU.add))
            chain(v.tensor_tensor(cnt[:, :], cnt[:, :], base[:, :], ALU.add))
            chain(cp(cnt_i[:, :], cnt[:, :]))
            chain(v.tensor_scalar(cnt_i[:, :], cnt_i[:, :], 7, None, ALU.logical_shift_right))
            chain(cp(ntl[:, :], cnt_i[:, :]))
            chain(v.tensor_scalar(jump[:, :], ntl[:, :], -float(P), float(ROWS), ALU.mult, ALU.add))
            chain(cp(tend[:, 0:1], ntl[:, 0:1]))
            for e in range(1, E):
                chain(v.tensor_tensor(tend[:, e:e + 1], tend[:, e - 1:e], ntl[:, e:e + 1], ALU.add))
            chain(v.memset(acc_e[:, :], 0.0))
            chain(v.tensor_scalar(acc_r[:, :], tnum[:, :], float(P), None, ALU.mult))
            for e in range(E - 1):
                chain(v.tensor_scalar(past[:, :], tnum[:, :], tend[:, e:e + 1], None, ALU.is_ge))
                v.tensor_tensor(acc_e[:, :], acc_e[:, :], past[:, :], ALU.add)
                chain(v.scalar_tensor_tensor(acc_r[:, :], past[:, :], jump[:, e:e + 1], acc_r[:, :], ALU.mult, ALU.add))
            cp(meta[:, 0, :], acc_r[:, :])
            v.tensor_scalar(meta[:, 1, :], acc_e[:, :], float(W13), None, ALU.mult)
            chain(v.tensor_scalar(meta[:, 2, :], acc_e[:, :], float(W2C), float(W2B), ALU.mult, ALU.add))
            v.memset(hb[:, H:KC * KH], 0.0).then_inc(s_meta, 1)

            def low_x(i, s):
                dve.wait_ge(a_x, i + 1)
                v.scalar_tensor_tensor(xTl[:, s, :, :], ps[:, 6, 0:C].rearrange("p (k n) -> p k n", k=2), SX,
                                       xTh[:, s, :, :],
                                       ALU.mult, ALU.subtract).then_inc(d_x, 1)

            def low_h(i):
                for c in range(2):
                    dve.wait_ge(a_t, i * 2 + c + 1)
                    if c == 0:
                        if later(i):
                            dve.wait_ge(p_y, i)
                    v.tensor_tensor(hTl[0:KH, 3 * c:3 * c + 3, :],
                                    ps[0:KH, 4 + c, 0:3 * P].rearrange("p (j n) -> p j n", j=3),
                                    hTh[0:KH, 3 * c:3 * c + 3, :], ALU.subtract).then_inc(d_t, 1)

            def gated(i, c):
                dve.wait_ge(a_s, i * 2 + c + 1)
                if later(i * 2):
                    dve.wait_ge(p_t, i * 2)
                v.scalar_tensor_tensor(hb[:, c * HC:(c + 1) * HC], ps[:, 2 * c + 1, 0:HC], SH / (SX * SW),
                                       sg[:, c, :], ALU.mult, ALU.mult).then_inc(d_h, 1)

            def weighed(i, s, turn):
                dve.wait_ge(p_y, i + 1)
                if later(i * 16):
                    dve.wait_ge(s_acc, i * 16)
                dve.wait_ge(s_slot[s], turn * 16 + 16)
                gate = slotsf[:, i, 1:2] if isinstance(i, int) else slotsf[:, ds(i, 1), 1]
                v.tensor_scalar(yg, ps[:, 7, 0:C], gate, 1.0 / (SH * SW), ALU.mult, ALU.mult).then_inc(d_y, 1)

            low_x(0, 0)
            gated(0, 0)
            low_x(1, 1)
            gated(0, 1)
            def tiles(it):
                for o in range(2):
                    i = it * 2 + 1 + o
                    low_h(i - 1)
                    gated(i, 0)
                    low_x(i + 1, o)
                    gated(i, 1)
                    weighed(i - 1, o, it)

            turns(dve, tiles, FT // 2)
            low_h(FT - 1)
            weighed(FT - 1, (FT - 1) % 2, FT // 2)


def kernel(**inputs):
    import numpy as np
    import concourse.bacc as bacc
    from concourse.bass_utils import run_bass_kernel_spmd

    a = {k: np.asarray(v) for k, v in inputs.items()}
    pad = np.pad
    src = pad(a["src"], (0, ET * P - EDGES), constant_values=DUMP)
    dst = pad(a["dst"], (0, ET * P - EDGES), constant_values=N - 1)
    w1, w3 = (a[n].transpose(0, 2, 1).reshape(E, 2, P, 2, 1, HC) for n in ("L0_ffn_w1", "L0_ffn_w3"))
    w13 = np.concatenate([w1, w3], axis=4).reshape(E * 2, P, 4 * HC).transpose(1, 0, 2).reshape(P, -1)
    w2 = pad(a["L0_ffn_w2"].transpose(0, 2, 1), ((0, 0), (0, KC * KH - H), (0, 0))).reshape(E * KC, KH, C)
    w2 = pad(w2, ((0, 0), (0, P - KH), (0, 0))).transpose(1, 0, 2).reshape(P, -1)
    wall = np.concatenate([w13, w2], axis=1).reshape(P, EG, WCH).transpose(1, 0, 2)
    arrays = {
        "x": pad(a["x"], ((0, ALLR - N), (0, 0))),
        "srcT": src.reshape(ET, P).T, "dstT": dst.reshape(ET, P).T, "src_rows": src.reshape(P, ET),
        "gw1t": a["L0_gnn_W1"].T, "gb1t": a["L0_gnn_b1"].reshape(GH // P, P).T,
        "gw2": a["L0_gnn_W2"], "gb2": a["L0_gnn_b2"].reshape(1, C),
        "rwt": a["L0_ffn_router_w"].T, "wall": wall,
    }
    arrays = {f"{k}_dram": np.ascontiguousarray(v) for k, v in arrays.items()}
    nc = bacc.Bacc("TRN2", target_bir_lowering=False, num_devices=1)
    args = [nc.dram_tensor(k, v.shape, mybir.dt.from_np(v.dtype), kind="ExternalInput").ap()
            for k, v in arrays.items()]
    out = nc.dram_tensor("out_dram", (ALLR, C), mybir.dt.float32, kind="ExternalOutput").ap()
    gnn_moe(nc, *args, out)
    r = run_bass_kernel_spmd(nc, [arrays], core_ids=[0])
    return r.results[0]["out_dram"][0:N]
```

```python
import concourse.bass as bass
from concourse import mybir
from contextlib import ExitStack

RMAX = bass.bass_isa.ReduceOp.max

P = 128
N, C, H, E = 6250, 256, 682, 8
GH = 512
NT = (N + P - 1) // P
ROWS = NT * P
DUMP = ROWS
ALLR = ROWS + P
EDGES = 106250
GT = 8
EG = (EDGES + P * GT - 1) // (P * GT)
ET = EG * GT
QT = 4
NCOPY = 4
TG = 7
NG = NT // TG
HB = 3
NP = (TG + 1) // 2
FT = (2 * ROWS + E * (P - 1)) // P
MT = FT + 3
TAB = (E - 1) * ROWS + MT * P
HC = 341
KC = 6
KH = 114
W13 = 2 * 4 * HC
W2C = KC * C
W2B = E * W13
WCOLS = W2B + E * W2C
WCH = WCOLS // EG
SY, SX, SW, SH = 64.0, 64.0, 64.0, 4.0
EPS = 1e-5

assert NT == TG * NG and WCH * EG == WCOLS and EG % 2 == 0 and FT % 2 == 1 and NG == 7


def gnn_moe(nc, x, srcT, dstT, src_rows, gw1t, gb1t, gw2, gb2, rwt, wall, out):
    f32, f16, bf16 = mybir.dt.float32, mybir.dt.float16, mybir.dt.bfloat16
    i32, u32 = mybir.dt.int32, mybir.dt.uint32
    ALU, ACT, AX = mybir.AluOpType, mybir.ActivationFunctionType, mybir.AxisListType
    ds = bass.ds
    Offset = bass.IndirectOffsetOnAxis

    dram = lambda name, shape, dt: nc.dram_tensor(name, shape, dt).ap()
    agg = [dram(f"agg{r}", (ALLR, C), f32) for r in range(NCOPY)]
    yhl = dram("yhl", (ALLR, 2 * C), f16)
    xhat_d = dram("xhat_d", (ALLR, C), f32)
    srow_d = dram("srow_d", (2, ET * P), f16)
    table = dram("table", (TAB, 2), i32)
    tiled = lambda t: t.rearrange("(t p) c -> p t c", p=P)
    x_t, out_t, yhl_t, xhat_t = tiled(x), tiled(out), tiled(yhl), tiled(xhat_d)
    agg_t = [tiled(a) for a in agg]

    with ExitStack() as ctx:
        sb = lambda name, shape, dt: ctx.enter_context(nc.sbuf_tensor(name, shape, dt))
        sem = lambda name: ctx.enter_context(nc.semaphore(name))

        WH = sb("WH", [P, WCOLS], f16)
        WL = sb("WL", [P, WCOLS], f16)
        WHf = WH[:, :].bitcast(f32)
        x_all = WHf[:, 0:NT * C].rearrange("p (t c) -> p t c", c=C)
        zeros = WHf[:, NT * C:NT * C + 2560]
        y_all = WL[:, 0:NT * 2 * C].rearrange("p (t c) -> p t c", c=2 * C)
        WLi = WL[:, :].bitcast(i32)
        T0 = NT * C
        tab_init = WLi[:, T0:T0 + 2 * (TAB // P)].rearrange("p (t w) -> p t w", w=2)
        T1 = T0 + 2 * (TAB // P)
        srow_i = WLi[:, T1:T1 + ET]
        srow_s = WLi[:, T1 + ET:T1 + 2 * ET]
        srow_h = WL[:, 2 * (T1 + 2 * ET):2 * (T1 + 2 * ET) + 2 * ET].rearrange("p (w t) -> p w t", w=2)
        assert 2 * (T1 + 2 * ET) + 2 * ET <= WCOLS and NT * C + 2560 <= WCOLS // 2

        iota_i = sb("iota_i", [P, P], i32)
        iota_f = sb("iota_f", [P, P], f32)
        iota_h = sb("iota_h", [P, P], f16)
        pcol_i = sb("pcol_i", [P, 1], i32)
        pcol = sb("pcol", [P, 1], f32)
        ident = sb("ident", [P, P], f32)
        before = sb("before", [P, P], f16)
        ones_h = sb("ones_h", [P, P], f16)
        ones_r = sb("ones_r", [1, P], f32)
        ones_b = sb("ones_b", [3, P], bf16)
        mix = sb("mix", [2, P], f16)
        pow_i = sb("pow_i", [P, 1], i32)
        pow_b = sb("pow_b", [P, 1], bf16)
        thr = sb("thr", [P, 1], f32)
        dumpcol = sb("dumpcol", [P, 1], f32)

        src_i = sb("src_i", [P, ET], i32)
        src_f = sb("src_f", [P, ET], f32)
        dst_i = sb("dst_i", [P, ET], i32)
        loc_f = sb("loc_f", [P, ET], f32)
        ext = sb("ext", [P, 2, EG], f32)
        exta = sb("exta", [P, 2, EG], f32)
        far = sb("far", [P, EG], f32)
        keep = sb("keep", [P, 2], f32)
        win_i = sb("win_i", [P, EG], i32)
        wide_f = sb("wide_f", [P, 1], f32)
        wide_i = sb("wide_i", [P, 1], i32)

        w12 = sb("w12", [P, 2, C], f32)
        b12 = sb("b12", [1, C], f32)
        brows = sb("brows", [3, C], bf16)
        b1col = sb("b1col", [P, 4], f32)
        b2row = sb("b2row", [1, C], f32)
        rw_sb = sb("rw_sb", [P, 2, E], f32)

        ROOM = 11520
        room = sb("room", [P, ROOM], f32)
        cur = [0]

        def take(words, dt, pattern=None, **sizes):
            v = room[:, cur[0]:cur[0] + words]
            cur[0] += words
            assert cur[0] <= ROOM, cur[0]
            if dt != f32:
                v = v.bitcast(dt)
            return v.rearrange(pattern, **sizes) if pattern else v

        ybuf = take(2 * GT * C, f16, "p (s k c) -> p s k c", s=2, k=GT)
        obuf = take(2 * GT * C, f32, "p (s k c) -> p s k c", s=2, k=GT)
        srow = take(GT * P, f16, "p (s n) -> p s n", s=2)
        wstage = take(2 * WCH, f32, "p (s n) -> p s n", s=2)
        eqb = take(QT * P, bf16, "p (q n) -> p q n", q=2)
        oneh = take(GT * P // 2, bf16, "p (k n) -> p k n", k=GT)
        msel = take(QT * P, f16, "p (q n) -> p q n", q=2)
        isdup = take(GT, f32)
        away = take(GT, f32)
        eidx = take(2 * GT, i32, "p (s k) -> p s k", s=2)
        gidx_b = take(1, i32)
        gw_a = room[:, 2 * GT * C:2 * GT * C + 8 * C].rearrange("p (j c) -> p j c", c=C)
        bsplit = room[0:1, 0:3 * C // 2].bitcast(bf16).rearrange("p (n c) -> p n c", n=3)
        cur[0] = 0
        hsum = take(HB * TG * C, f32, "p (s t c) -> p s t c", s=HB, t=TG)
        xres = take(2 * TG * C, f32, "p (s t c) -> p s t c", s=2, t=TG)
        xhat = take(TG * C, f32, "p (t c) -> p t c", t=TG)
        pair = lambda t: t[:, 0:2 * C].rearrange("p (t k n) -> p t k n", t=2, k=2)
        xT = [pair(take(2 * C, f32)), pair(src_i[:, :].bitcast(f32))]
        hT = [pair(loc_f), pair(dst_i[:, :].bitcast(f32))]
        cur[0] = 0
        xg = take(2 * C, f32, "p (s c) -> p s c", s=2)
        xTh = take(C, f16, "p (s k n) -> p s k n", s=2, k=2)
        xTl = take(C, f16, "p (s k n) -> p s k n", s=2, k=2)
        sg = take(2 * HC, f32, "p (s n) -> p s n", s=2)
        hb = take(KC * KH, f32)
        hTh = take(KC * P // 2, f16, "p (j n) -> p j n", j=KC)
        hTl = take(KC * P // 2, f16, "p (j n) -> p j n", j=KC)
        yg = take(C, f32)
        slots = take(2 * MT, i32, "p (i w) -> p i w", w=2)
        slotsf = slots.bitcast(f32)

        bst = sb("bst", [P, TG, 6], f32)
        mv = sb("mv", [P, TG, 2], f32)
        rstd = sb("rstd", [P, TG], f32)
        mx = sb("mx", [P, TG, 8], f32)
        mxi = sb("mxi", [P, TG, 8], u32)
        sel = sb("sel", [P, 2, TG], f32)
        dif = sb("dif", [P, TG, 8], f32)
        exs = sb("exs", [P, TG, 8], f32)
        prb = sb("prb", [P, 4, TG], f32)
        oneh_e = sb("oneh_e", [P, 2, TG, E], f32)
        picked = sb("picked", [P, TG, E], f16)
        rank = sb("rank", [P, TG, E], f32)
        prod = sb("prod", [P, 2, TG, E], f32)
        place = sb("place", [P, 2, TG], f32)
        place_i = sb("place_i", [P, 2, 2, TG], i32)
        base = sb("base", [P, E], f32)
        tok = sb("tok", [P, TG], f32)
        load_ = sb("load_", [P, 2, TG, 2, 2], i32)
        loadf = load_[:, :, :, :, :].bitcast(f32)
        cnt = sb("cnt", [P, E], f32)
        cnt_i = sb("cnt_i", [P, E], i32)
        ntl = sb("ntl", [P, E], f32)
        tend = sb("tend", [P, E], f32)
        jump = sb("jump", [P, E], f32)
        tnum_i = sb("tnum_i", [P, MT], i32)
        tnum = sb("tnum", [P, MT], f32)
        past, acc_e, acc_r = (src_f[:, k * MT:(k + 1) * MT] for k in range(3))
        meta = sb("meta", [P, 3, MT], i32)
        gidx = sb("gidx", [P, 2], i32)
        sidx = sb("sidx", [P, 1], i32)

        ps = ctx.enter_context(nc.psum_tensor("ps", [P, 8, 512], f32))

        s_in = sem("s_in")
        s_x = sem("s_x")
        s_gw = sem("s_gw")
        s_pool = sem("s_pool")
        s_zero = sem("s_zero")
        s_const = sem("s_const")
        s_dve = sem("s_dve")
        s_tab = sem("s_tab")
        s_srow = sem("s_srow")
        s_ext = sem("s_ext")
        s_ar = sem("s_ar")
        s_edges = sem("s_edges")
        s_w12 = sem("s_w12")
        s_w12c = sem("s_w12c")
        s_var = sem("s_var")
        s_sd = sem("s_sd")
        s_yn = sem("s_yn")
        s_yh = sem("s_yh")
        s_yl = sem("s_yl")
        s_init = sem("s_init")
        s_win = [sem(f"s_win{s}") for s in range(2)]
        s_row = [sem(f"s_row{s}") for s in range(2)]
        s_wst = [sem(f"s_wst{s}") for s in range(2)]
        s_bc = sem("s_bc")
        s_eq = sem("s_eq")
        s_one = sem("s_one")
        s_idx = sem("s_idx")
        s_sel = sem("s_sel")
        s_selc = sem("s_selc")
        s_o = sem("s_o")
        s_ob = sem("s_ob")
        s_wcp = sem("s_wcp")
        s_free = sem("s_free")
        s_add = [sem(f"s_add{r}") for r in range(NCOPY)]
        s_wh = sem("s_wh")
        s_wl = sem("s_wl")
        s_bias = sem("s_bias")
        s_bias3 = sem("s_bias3")
        s_h0 = [sem(f"s_h0{s}") for s in range(HB)]
        s_h3 = [sem(f"s_h3{s}") for s in range(HB)]
        s_xr = [sem(f"s_xr{s}") for s in range(2)]
        s_ht = sem("s_ht")
        s_htc = sem("s_htc")
        s_z = sem("s_z")
        s_x2 = sem("s_x2")
        s_xn = sem("s_xn")
        s_xt = sem("s_xt")
        s_xtc = sem("s_xtc")
        s_lg = sem("s_lg")
        s_mx = sem("s_mx")
        s_ex = sem("s_ex")
        s_pk = sem("s_pk")
        s_rk = sem("s_rk")
        s_pos = sem("s_pos")
        s_scat = [sem(f"s_scat{s}") for s in range(2)]
        s_st = [sem(f"s_st{s}") for s in range(2)]
        s_sth = sem("s_sth")
        s_meta = sem("s_meta")
        s_slot = [sem(f"s_slot{s}") for s in range(2)]
        s_cp = sem("s_cp")
        s_xg = [sem(f"s_xg{s}") for s in range(2)]
        p_x = sem("p_x")
        a_x = sem("a_x")
        d_x = sem("d_x")
        p_h = sem("p_h")
        a_s = sem("a_s")
        d_h = sem("d_h")
        p_t = sem("p_t")
        a_t = sem("a_t")
        d_t = sem("d_t")
        p_y = sem("p_y")
        d_y = sem("d_y")
        s_acc = sem("s_acc")
        block = ctx.enter_context(nc.Block())

        ZW = 2560
        INIT_ALL = 16 * ((NCOPY - 1) * (ALLR // P * C // ZW) + 3 + 1 + 1 + 1 + 2 * NG)

        def part(v, i, n=1):
            return v[:, i:i + n] if isinstance(i, int) else v[:, ds(i, n)]

        def apart(eng):
            eng.nop(nofuse=True)

        def later(value):
            return not isinstance(value, int) or value > 0

        def turns(eng, body, count):
            body(0)
            with eng.Fori(1, count) as turn:
                body(turn)

        class Chain:

            def __init__(self, eng, s):
                self.eng, self.s, self.n, self.turn, self.start, self.steps = eng, s, 0, 0, 0, 0

            def __call__(self, ins):
                ins.then_inc(self.s, 1)
                self.n += 1
                self.eng.wait_ge(self.s, self.turn * self.steps + self.n)
                if self.steps:
                    apart(self.eng)

            def enter(self, turn, steps):
                if not self.steps:
                    self.start = self.n
                self.turn, self.steps, self.n = turn, steps, self.start

            def leave(self, count):
                assert self.n - self.start == self.steps, self.n - self.start
                self.n, self.turn, self.steps = self.start + count * self.steps, 0, 0

        @block.sync
        def _(sp):
            sp.dma_start(src_i[:, :], srcT).then_inc(s_in, 16)
            sp.dma_start(dst_i[:, :], dstT).then_inc(s_in, 16)
            sp.dma_start(srow_i, src_rows).then_inc(s_in, 16)
            for g in range(NG):
                t = slice(g * TG, (g + 1) * TG)
                sp.dma_start(x_all[:, t, :], x_t[:, t, :]).then_inc(s_x, 16)
            sp.dma_start(gw_a[:, 0:4, :], gw1t.rearrange("(j p) c -> p j c", p=P)).then_inc(s_gw, 16)
            sp.dma_start(gw_a[:, 4:8, :], gw2.rearrange("(j p) c -> p j c", p=P)).then_inc(s_gw, 16)
            sp.dma_start(b1col[:, :], gb1t).then_inc(s_gw, 16)
            sp.dma_start(b2row[:, :], gb2).then_inc(s_gw, 16)
            sp.dma_start(rw_sb[:, :, :], rwt.rearrange("(k p) e -> p k e", p=P)).then_inc(s_gw, 16)

            sp.wait_ge(s_zero, 1)
            for r in range(1, NCOPY):
                flat = agg[r].rearrange("(p t) c -> p (t c)", p=P)
                for k in range(ALLR // P * C // ZW):
                    sp.dma_start(flat[:, k * ZW:(k + 1) * ZW], zeros).then_inc(s_init, 16)
            for t in (agg[0], xhat_d, out):
                sp.dma_start(t[DUMP:ALLR, :], zeros[:, 0:C]).then_inc(s_init, 16)
            sp.dma_start(yhl[DUMP:ALLR, :], zeros[:, 0:C].bitcast(f16)).then_inc(s_init, 16)
            sp.wait_ge(s_tab, 1)
            sp.dma_start(table.rearrange("(p t) w -> p t w", p=P), tab_init).then_inc(s_init, 16)
            sp.wait_ge(s_srow, 1)
            sp.dma_start(srow_d.rearrange("w (p t) -> p w t", p=P), srow_h).then_inc(s_init, 16)
            for g in range(NG):
                t = slice(g * TG, (g + 1) * TG)
                sp.wait_ge(s_yl, g + 1)
                sp.dma_start(agg_t[0][:, t, :], x_all[:, t, :]).then_inc(s_init, 16)
                sp.dma_start(yhl_t[:, t, :], y_all[:, t, :]).then_inc(s_init, 16)

            sp.wait_ge(s_init, INIT_ALL)
            sp.wait_ge(s_edges, 1)
            sp.wait_ge(s_bias3, 16)
            wide = sp.value_load(wide_i[0:1, 0:1], min_val=0, max_val=1)

            def group_loads(g, s):
                win = sp.value_load(part(win_i[0:1, :], g), min_val=0, max_val=N - 1)
                sp.dma_start(srow[0:2, s, :], part(srow_d, g * GT * P, GT * P)).then_inc(s_row[s], 16)
                with sp.If(wide == 0):
                    for k in range(GT):
                        sp.dma_start(ybuf[16 * k:16 * k + 16, s, 0, :],
                                     yhl[ds(win + 16 * k, 16), :]).then_inc(s_win[s], 16)
                sp.dma_start(wstage[:, s, :], wall[g] if isinstance(g, int)
                             else wall[ds(g, 1), :, :].rearrange("a p n -> p (a n)")).then_inc(s_wst[s], 16)

            for g in range(2):
                group_loads(g, g)
            with sp.Fori(0, EG // 2 - 1) as it:
                for s in range(2):
                    g = it * 2 + s
                    sp.wait_ge(s_ob, g * 4 + 4)
                    apart(sp)
                    sp.wait_ge(s_wl, g + 1)
                    apart(sp)
                    group_loads(g + 2, s)

            for r in range(NCOPY):
                sp.wait_ge(s_add[r], 16 * (ET // NCOPY))
            sp.wait_ge(s_wl, EG)

            def sum_load(g):
                if g >= HB:
                    sp.wait_ge(s_ht, (g - HB + 1) * NP)
                sp.dma_start(hsum[:, g % HB, :, :], agg_t[0][:, g * TG:(g + 1) * TG, :])\
                    .then_inc(s_h0[g % HB], 16)

            sum_load(0)
            for g in range(NG):
                s, t = g % 2, slice(g * TG, (g + 1) * TG)
                if g + 1 < NG:
                    sum_load(g + 1)
                if g >= 2:
                    sp.wait_ge(s_xn, (g - 1) * TG)
                    sp.wait_ge(s_st[s], g // 2 * 16)
                sp.dma_start(xres[:, s, :, :], x_t[:, t, :]).then_inc(s_xr[s], 16)

            sp.wait_ge(s_meta, 1)
            for s in range(2):
                sp.wait_ge(s_scat[s], 16 * 2 * TG * ((NG + 1 - s) // 2))
                sp.wait_ge(s_st[s], 16 * ((NG + 1 - s) // 2))
            sp.wait_ge(s_sth, 16 * NG)
            def slot_loads(it):
                for s in range(2):
                    i = it * 2 + s
                    row = sp.value_load(meta[0:1, 0, ds(i, 1)], min_val=0, max_val=TAB - P)
                    if later(it * 16):
                        sp.wait_ge(s_slot[s], it * 16)
                    apart(sp)
                    sp.dma_start(slots[:, ds(i, 1), :],
                                 table[ds(row, P), :].rearrange("(a p) w -> p a w", p=P)).then_inc(s_slot[s], 16)

            turns(sp, slot_loads, MT // 2)
            for s in range(2):
                sp.wait_ge(s_slot[s], MT // 2 * 16)
        @block.gpsimd
        def _(pool):
            chain = Chain(pool, s_pool)
            chain(pool.memset(zeros, 0.0))
            chain(pool.iota(tab_init, pattern=[[1, TAB // P], [0, 2]], base=0, channel_multiplier=TAB // P))
            chain(pool.memset(tab_init[:, :, 1:2], 0))
            pool.sem_inc(s_zero, 1)
            chain(pool.iota(iota_i[:, :], pattern=[[1, P]], base=0, channel_multiplier=0))
            chain(pool.iota(pcol_i[:, :], pattern=[[0, 1]], base=0, channel_multiplier=1))
            chain(pool.iota(tnum_i[:, :], pattern=[[1, MT]], base=0, channel_multiplier=0))
            chain(pool.iota(pow_i[:, :], pattern=[[0, 1]], base=127 + 63, channel_multiplier=-1))
            chain(pool.memset(ident[:, :], 0.0))
            chain(pool.affine_select(out=ident[:, :], in_=ident[:, :], compare_op=ALU.not_equal, fill=1.0,
                                     base=0, pattern=[[-1, P]], channel_multiplier=1))
            chain(pool.memset(ones_h[:, :], 1.0))
            chain(pool.affine_select(out=before[:, :], in_=ones_h[:, :], compare_op=ALU.is_gt, fill=0.0,
                                     base=0, pattern=[[1, P]], channel_multiplier=-1))
            chain(pool.memset(ones_r[:, :], 1.0))
            chain(pool.memset(ones_b[:, :], 1.0))
            chain(pool.memset(mix[:, :], 1.0))
            chain(pool.memset(mix[0:1, :], 64.0))
            pool.sem_inc(s_const, 1)
            pool.wait_ge(s_ext, 1)
            pool.partition_all_reduce(exta[:, :, :].rearrange("p a g -> p (a g)"),
                                      ext[:, :, :].rearrange("p a g -> p (a g)"), P, RMAX).then_inc(s_ar, 1)

            pool.wait_ge(s_init, INIT_ALL)
            pool.wait_ge(s_edges, 1)
            wide = pool.value_load(wide_i[0:1, 0:1], min_val=0, max_val=1)
            def edge_groups(it):
                for s in range(2):
                    g = it * 2 + s
                    with pool.If(wide == 1):
                        if later(g * 4):
                            pool.wait_ge(s_ob, g * 4)
                        for k in range(GT):
                            if later((it * GT + k) * 16):
                                pool.wait_ge(s_win[s], (it * GT + k) * 16)
                            pool.tensor_copy(gidx_b, dst_i[:, ds(g * GT + k, 1)]).then_inc(s_wcp, 1)
                            pool.wait_ge(s_wcp, g * GT + k + 1)
                            apart(pool)
                            pool.indirect_dma_start(ybuf[:, s, k, :], None, yhl[:, :],
                                                    Offset(ap=gidx_b, axis=0)).then_inc(s_win[s], 16)
                        pool.wait_ge(s_win[s], (it + 1) * GT * 16)
                    pool.wait_ge(s_idx, g + 1)
                    for k in range(GT):
                        if k % 2 == 0:
                            pool.wait_ge(s_ob, g * 4 + k // 2 + 1)
                        r = k % NCOPY
                        if later((g * (GT // NCOPY) + k // NCOPY) * 16):
                            pool.wait_ge(s_add[r], (g * (GT // NCOPY) + k // NCOPY) * 16)
                        apart(pool)
                        pool.indirect_dma_start(agg[r][:, :], Offset(ap=eidx[:, s, k:k + 1], axis=0),
                                                obuf[:, s, k, :], None, bounds_check=ALLR - 1, oob_is_err=True,
                                                compute_op=ALU.add).then_inc(s_add[r], 16)
                        if k == NCOPY - 1:
                            pool.sem_inc(s_free, 1)

            turns(pool, edge_groups, EG // 2)
            for r in range(NCOPY):
                pool.wait_ge(s_add[r], 16 * (ET // NCOPY))

            def add_copy(g, r):
                s = g % HB
                if r == 1:
                    pool.wait_ge(s_h0[s], g // HB * 16 + 16)
                else:
                    pool.wait_ge(s_h3[s], (g // HB * (NCOPY - 1) + r - 1) * 16)
                pool.dma_start(hsum[:, s, :, :], agg_t[r][:, g * TG:(g + 1) * TG, :],
                               accum_op=ALU.add).then_inc(s_h3[s], 16)

            for step in range(NCOPY + HB - 1):
                for g in range(min(step + 1, HB + 1)):
                    if 1 <= step + 1 - g < NCOPY:
                        add_copy(g, step + 1 - g)
            for g in range(NG):
                pool.wait_ge(s_pos, g + 1)
                for t in range(TG):
                    for k in range(2):
                        pool.indirect_dma_start(table[:, :], Offset(ap=place_i[:, g % 2, k, t:t + 1], axis=0),
                                                load_[:, g % 2, t, k, :], None).then_inc(s_scat[g % 2], 16)
                    if g + HB + 1 < NG and t in (0, 3, 6):
                        add_copy(g + HB + 1, 1 + t // 3)

            def fetch(i, s, seen, done, copies):
                pool.wait_ge(s_slot[s], seen)
                if later(done):
                    pool.wait_ge(p_x, done)
                pool.tensor_copy(gidx[:, s:s + 1], slots[:, i, 0:1] if isinstance(i, int)
                                 else slots[:, ds(i, 1), 0]).then_inc(s_cp, 1)
                pool.wait_ge(s_cp, copies)
                apart(pool)
                pool.indirect_dma_start(xg[:, s, :], None, xhat_d[:, :],
                                        Offset(ap=gidx[:, s:s + 1], axis=0)).then_inc(s_xg[s], 16)

            def add_out(i, copies):
                if later(i * 16):
                    pool.wait_ge(s_acc, i * 16)
                pool.tensor_copy(sidx[:, :], slots[:, i, 0:1] if isinstance(i, int)
                                 else slots[:, ds(i, 1), 0]).then_inc(s_cp, 1)
                pool.wait_ge(s_cp, copies)
                pool.wait_ge(d_y, i + 1)
                apart(pool)
                pool.indirect_dma_start(out[:, :], Offset(ap=sidx[:, :], axis=0), yg, None,
                                        bounds_check=ALLR - 1, oob_is_err=True,
                                        compute_op=ALU.add).then_inc(s_acc, 16)

            pool.wait_ge(s_sth, 16 * NG)
            for s in range(2):
                pool.wait_ge(s_st[s], 16 * ((NG + 1 - s) // 2))
            for i in range(3):
                fetch(i, i % 2, i // 2 * 16 + 16, i - 1, i + 1)

            def tiles(it):
                for o in range(2):
                    i = it * 2 + 1 + o
                    fetch(i + 2, 1 - o, it * 16 + 32 + 16 * o, i + 1, it * 4 + 2 * o + 4)
                    add_out(i - 1, it * 4 + 2 * o + 5)

            turns(pool, tiles, FT // 2)
            add_out(FT - 1, 2 * FT + 2)
            pool.wait_ge(s_acc, 16 * FT)
            pool.wait_ge(s_xg[0], 16 * (FT // 2 + 2))
            pool.wait_ge(s_xg[1], 16 * (FT // 2 + 1))

        @block.tensor
        def _(pe):
            mm = nc.tensor.matmul

            pe.wait_ge(s_gw, 80)
            pe.wait_ge(s_const, 1)
            for k in range(2):
                for j in range(4):
                    mm(ps[:, k, 0:C], gw_a[:, j, k * P:(k + 1) * P], gw_a[:, 4 + j, :], start=j == 0, stop=j == 3)
            for j in range(4):
                mm(ps[0:1, 2, 0:C], b1col[:, j:j + 1], gw_a[:, 4 + j, :], start=j == 0, stop=False)
            mm(ps[0:1, 2, 0:C], ones_r[0:1, 0:1], b2row[:, :], start=False, stop=True).then_inc(s_w12, 1)
            pe.wait_ge(s_w12c, 1)

            pe.wait_ge(s_edges, 1)
            wide = pe.value_load(wide_i[0:1, 0:1], min_val=0, max_val=1)
            def edge_groups(it):
                for s in range(2):
                    g = it * 2 + s
                    pe.wait_ge(s_row[s], it * 16 + 16)
                    if later(g * 2):
                        pe.wait_ge(s_eq, g * 2)
                    for q in range(2):
                        mm(ps[:, q, :], mix[:, :], srow[0:2, s, q * QT * P:(q + 1) * QT * P],
                           start=True, stop=True).then_inc(s_bc, 1)
                    pe.wait_ge(s_one, g + 1)
                    if later(g):
                        pe.wait_ge(s_idx, g)
                    for q in range(2):
                        pe.wait_ge(s_eq, g * 2 + q + 1)
                        for k in range(QT):
                            e = eqb[:, q, k * P:(k + 1) * P]
                            mm(ps[:, 6, q * QT + k:q * QT + k + 1], e, pow_b[:, :], start=True, stop=True)
                        for k in range(QT):
                            e = eqb[:, q, k * P:(k + 1) * P]
                            last = mm(ps[:, 2 + q, k * P:(k + 1) * P], oneh[:, q * QT + k, :], e,
                                      start=True, stop=True)
                        last.then_inc(s_sel, 1)
                    pe.wait_ge(s_win[s], it * (16 * GT) + 16 * GT)
                    for j in range(GT // 2):
                        if j % 2 == 0:
                            pe.wait_ge(s_selc, g * 2 + j // 2 + 1)
                        if j >= 2:
                            pe.wait_ge(s_ob, g * 4 + j - 1)
                        for k in (2 * j, 2 * j + 1):
                            rows = ybuf[:, s, 0, :] if k == 0 else ybuf[:, s, ds(wide * k, 1), :]
                            m = msel[:, k // QT, (k % QT) * P:(k % QT + 1) * P]
                            for h in range(2):
                                y = rows[:, h * C:(h + 1) * C] if k == 0 else \
                                    rows[:, :, h * C:(h + 1) * C].rearrange("p a c -> p (a c)")
                                last = mm(ps[:, 4 + j % 2, (k % 2) * C:(k % 2 + 1) * C], m, y,
                                          start=h == 0, stop=h == 1)
                        last.then_inc(s_o, 1)

            turns(pe, edge_groups, EG // 2)
            def pair_of(j):
                return range(2 * j, min(2 * j + 2, TG))

            turned_to = [0]

            def gnn_out(g, pairs, ahead=True):
                def turn_sums(j):
                    n = g * NP + j
                    turned_to[0] = n + 1
                    if n >= 2:
                        pe.wait_ge(s_htc, n - 1)
                    for i, t in enumerate(pair_of(j)):
                        for k in range(2):
                            last = nc.tensor.transpose(ps[:, n % 2, (2 * i + k) * P:(2 * i + k + 1) * P],
                                                       hsum[:, g % HB, t, k * P:(k + 1) * P], ident[:, :])
                    last.then_inc(s_ht, 1)

                if pairs[0] == 0:
                    pe.wait_ge(s_h3[g % HB], (g // HB + 1) * 16 * (NCOPY - 1))
                if turned_to[0] == g * NP + pairs[0]:
                    turn_sums(pairs[0])
                if pairs[0] == 0 and g:
                    pe.wait_ge(s_x2, g)
                for j in range(*pairs):
                    if j + 1 < (NP if ahead else pairs[1]):
                        turn_sums(j + 1)
                    n = g * NP + j
                    pe.wait_ge(s_htc, n + 1)
                    for i, t in enumerate(pair_of(j)):
                        z = ps[:, 2 + j, i * C:(i + 1) * C]
                        for k in range(2):
                            mm(z, hT[n % 2][:, i, k, :], w12[:, k, :], start=k == 0, stop=False)
                        last = mm(z, ones_b[:, :], brows[:, :], start=False, stop=True)
                    last.then_inc(s_z, 1)

            def router(g):
                if g:
                    pe.wait_ge(s_mx, g)

                def turn_x(j):
                    n = g * NP + j
                    if n >= 2:
                        pe.wait_ge(s_xtc, n - 1)
                    for i, t in enumerate(pair_of(j)):
                        pe.wait_ge(s_xn, g * TG + t + 1)
                        for k in range(2):
                            last = nc.tensor.transpose(ps[:, n % 2, (2 * i + k) * P:(2 * i + k + 1) * P],
                                                       xhat[:, t, k * P:(k + 1) * P], ident[:, :])
                    last.then_inc(s_xt, 1)

                turn_x(0)
                for j in range(NP):
                    if j + 1 < NP:
                        turn_x(j + 1)
                    n = g * NP + j
                    pe.wait_ge(s_xtc, n + 1)
                    for i, t in enumerate(pair_of(j)):
                        for k in range(2):
                            last = mm(ps[:, 6, t * E:(t + 1) * E], xT[n % 2][:, i, k, :], rw_sb[:, k, :],
                                      start=k == 0, stop=k == 1)
                    last.then_inc(s_lg, 1)

            def ranks(g):
                pe.wait_ge(s_pk, g + 1)
                if g:
                    pe.wait_ge(s_pos, g)
                flat = picked[:, :, :].rearrange("p t e -> p (t e)")
                mm(ps[:, 7, 0:TG * E], before[:, :], flat, start=True, stop=False, skip_group_check=True)
                for d in range(1, TG):
                    mm(ps[:, 7, d * E:TG * E], ones_h[:, :], flat[:, 0:(TG - d) * E], start=False,
                       stop=d == TG - 1, skip_group_check=True)
                for t in range(TG):
                    last = mm(ps[:, 7, 64:64 + E], ones_h[:, :], picked[:, t, :], start=t == 0, stop=t == TG - 1)
                last.then_inc(s_rk, 1)

            pe.wait_ge(s_bias3, 16)
            gnn_out(0, (0, NP))
            gnn_out(1, (0, 2), False)
            router(0)
            gnn_out(1, (2, 3))
            ranks(0)
            gnn_out(1, (3, NP))
            gnn_out(2, (0, NP))
            router(1)
            for g in range(1, NG):
                if g + 2 < NG:
                    gnn_out(g + 2, (0, 1))
                ranks(g)
                if g + 2 < NG:
                    gnn_out(g + 2, (1, NP))
                if g + 1 < NG:
                    router(g + 1)

            def turn_tile(i, s, seen):
                pe.wait_ge(s_xg[s], seen)
                if later(i):
                    pe.wait_ge(d_x, i)
                for k in range(2):
                    last = nc.tensor.transpose(ps[:, 6, k * P:(k + 1) * P], xg[:, s, k * P:(k + 1) * P], ident[:, :])
                last.then_inc(p_x, 1)

            def hidden(i, s, halves, col, first):
                for c in halves:
                    if not first:
                        pe.wait_ge(d_h, i * 2 - 1 + c)
                    for k, (xp, wp) in enumerate(((xTh, WH), (xTh, WL), (xTl, WH))):
                        for kk in range(2):
                            for m in range(2):
                                o = kk * 4 * HC + c * 2 * HC + m * HC
                                last = mm(ps[:, 2 * c + m, 0:HC], xp[:, s, kk, :], wp[:, ds(col + o, HC)],
                                          start=k == 0 and kk == 0, stop=k == 2 and kk == 1)
                    last.then_inc(p_h, 1)

            def turn_h(i):
                pe.wait_ge(d_h, i * 2 + 2)
                if later(i * 2):
                    pe.wait_ge(d_t, i * 2)
                for j in range(KC):
                    last = nc.tensor.transpose(ps[0:KH, 4 + j // 3, (j % 3) * P:(j % 3 + 1) * P],
                                               hb[:, j * KH:(j + 1) * KH], ident[:, :])
                    if j % 3 == 2:
                        last.then_inc(p_t, 1)

            def output(i, col):
                pe.wait_ge(d_t, i * 2 + 2)
                if later(i):
                    pe.wait_ge(d_y, i)
                for j in range(KC):
                    for n, (hp, wp) in enumerate(((hTh, WH), (hTh, WL), (hTl, WH))):
                        last = mm(ps[:, 7, 0:C], hp[0:KH, j, :], wp[0:KH, ds(col + j * C, C)],
                                  start=j == 0 and n == 0, stop=j == KC - 1 and n == 2)
                last.then_inc(p_y, 1)

            def column(row, i):
                v = meta[0:1, row, i:i + 1] if isinstance(i, int) else meta[0:1, row, ds(i, 1)]
                return pe.value_load(v, min_val=0 if row == 1 else W2B,
                                     max_val=(E - 1) * W13 if row == 1 else W2B + (E - 1) * W2C)

            pe.wait_ge(s_meta, 1)
            turn_tile(0, 0, 16)
            pe.wait_ge(d_x, 1)
            hidden(0, 0, (0,), column(1, 0), True)
            turn_tile(1, 1, 16)
            hidden(0, 0, (1,), column(1, 0), True)
            def tiles(it):
                for o in range(2):
                    i = it * 2 + 1 + o
                    w13, w2 = column(1, i), column(2, i - 1)
                    turn_h(i - 1)
                    pe.wait_ge(d_x, i + 1)
                    hidden(i, 1 - o, (0,), w13, False)
                    turn_tile(i + 1, o, it * 16 + 32)
                    hidden(i, 1 - o, (1,), w13, False)
                    output(i - 1, w2)

            turns(pe, tiles, FT // 2)
            turn_h(FT - 1)
            output(FT - 1, column(2, FT - 1))

        @block.scalar
        def _(act):
            copy = lambda o, i, scale=1.0: nc.scalar.activation(o, i, ACT.Copy, scale=scale)
            act.wait_ge(s_w12, 1)
            copy(w12[:, :, :], ps[:, 0:2, 0:C])
            copy(b12[:, :], ps[0:1, 2, 0:C]).then_inc(s_w12c, 1)
            act.wait_ge(s_bias, 1)
            act.dma_start(brows[:, :], bsplit).then_inc(s_bias3, 16)

            def roots(n):
                act.wait_ge(s_var, n)
                nc.scalar.activation(rstd[:, :], mv[:, :, 1], ACT.Sqrt).then_inc(s_sd, 1)

            with act.Fori(0, NG) as g:
                roots(g + 1)
                act.wait_ge(s_yn, g + 1)
                copy(y_all[:, ds(g * TG, TG), 0:C], x_all[:, ds(g * TG, TG), :], SY).then_inc(s_yh, 1)

            act.wait_ge(s_init, INIT_ALL)
            def edge_groups(it):
                for s in range(2):
                    g = it * 2 + s
                    for q in range(2):
                        act.wait_ge(s_sel, g * 2 + q + 1)
                        copy(msel[:, q, :], ps[:, 2 + q, :]).then_inc(s_selc, 1)
                    if later(g):
                        act.wait_ge(s_free, g)
                    for j in range(GT // 2):
                        act.wait_ge(s_o, g * 4 + j + 1)
                        copy(obuf[:, s, 2 * j:2 * j + 2, :], ps[:, 4 + j % 2, :].rearrange("p (k c) -> p k c", k=2),
                             1.0 / SY).then_inc(s_ob, 1)
                    act.wait_ge(s_wst[s], it * 16 + 16)
                    copy(WH[:, ds(g * WCH, WCH)], wstage[:, s, :], SW).then_inc(s_wh, 1)

            turns(act, edge_groups, EG // 2)
            def turned(g, pairs, ready, read, out_, done):
                for j in range(*pairs):
                    n = g * NP + j
                    act.wait_ge(ready, n + 1)
                    if n >= 2:
                        act.wait_ge(read, n - 1)
                    w = min(2, TG - 2 * j)
                    copy(out_[n % 2][:, 0:w, :, :], ps[:, n % 2, 0:w * C]
                         .rearrange("p (t k n) -> p t k n", t=w, k=2)).then_inc(done, 1)

            def sums(g, pairs):
                turned(g, pairs, s_ht, s_z, hT, s_htc)

            def router_in(g, pairs):
                turned(g, pairs, s_xt, s_lg, xT, s_xtc)

            def store_x2(g):
                act.wait_ge(s_x2, g + 1)
                act.dma_start(out_t[:, g * TG:(g + 1) * TG, :], xres[:, g % 2, :, :]).then_inc(s_st[g % 2], 16)

            def store_xhat(g):
                act.dma_start(xhat_t[:, g * TG:(g + 1) * TG, :], xhat).then_inc(s_sth, 16)

            def exponentials(g):
                act.wait_ge(s_mx, g + 1)
                nc.scalar.activation(exs[:, :, :], dif[:, :, :], ACT.Exp).then_inc(s_ex, 1)

            act.wait_ge(s_bias3, 16)
            sums(0, (0, NP))
            store_x2(0)
            sums(1, (0, 2))
            roots(NG + 1)
            router_in(0, (0, NP))
            store_xhat(0)
            sums(1, (2, 3))
            exponentials(0)
            sums(1, (3, NP))
            store_x2(1)
            sums(2, (0, 2))
            roots(NG + 2)
            sums(2, (2, NP))
            router_in(1, (0, 2))
            store_x2(2)
            router_in(1, (2, NP))
            roots(NG + 3)
            for g in range(1, NG):
                store_xhat(g)
                if g + 2 < NG:
                    sums(g + 2, (0, 1))
                exponentials(g)
                if g + 2 < NG:
                    sums(g + 2, (1, NP))
                if g + 1 < NG:
                    router_in(g + 1, (0, 2))
                if g + 2 < NG:
                    store_x2(g + 2)
                if g + 1 < NG:
                    router_in(g + 1, (2, NP))
                if g + 2 < NG:
                    roots(NG + g + 3)

            def high_x(i, s):
                act.wait_ge(p_x, i + 1)
                if not isinstance(i, int) or i > 1:
                    act.wait_ge(p_h, i * 2 - 2)
                copy(xTh[:, s, :, :], ps[:, 6, 0:C].rearrange("p (k n) -> p k n", k=2), SX).then_inc(a_x, 1)

            def high_h(i):
                for c in range(2):
                    act.wait_ge(p_t, i * 2 + c + 1)
                    if c == 0:
                        if later(i):
                            act.wait_ge(p_y, i)
                    copy(hTh[0:KH, 3 * c:3 * c + 3, :],
                         ps[0:KH, 4 + c, 0:3 * P].rearrange("p (j n) -> p j n", j=3)).then_inc(a_t, 1)

            def silu(i, c, first=False):
                act.wait_ge(p_h, i * 2 + c + 1)
                if not first:
                    act.wait_ge(d_h, i * 2 - 1 + c)
                nc.scalar.activation(sg[:, c, :], ps[:, 2 * c, 0:HC], ACT.Silu,
                                     scale=1.0 / (SX * SW)).then_inc(a_s, 1)

            high_x(0, 0)
            silu(0, 0, True)
            high_x(1, 1)
            silu(0, 1, True)
            def tiles(it):
                for o in range(2):
                    i = it * 2 + 1 + o
                    high_h(i - 1)
                    silu(i, 0)
                    high_x(i + 1, o)
                    silu(i, 1)

            turns(act, tiles, FT // 2)
            high_h(FT - 1)

        @block.vector
        def _(dve):
            v = nc.vector
            chain = Chain(dve, s_dve)
            cp = v.tensor_copy
            dve.wait_ge(s_zero, 1)
            t0 = tab_init[:, :, 0]
            chain(v.tensor_scalar(t0, t0, P - 1, None, ALU.bitwise_and))
            v.tensor_scalar(t0, t0, DUMP, None, ALU.add).then_inc(s_tab, 1)
            dve.wait_ge(s_in, 48)
            chain(v.tensor_scalar(srow_s, srow_i, 6, None, ALU.logical_shift_right))
            chain(cp(srow_h[:, 0, :], srow_s))
            chain(v.tensor_scalar(srow_s, srow_i, 63, None, ALU.bitwise_and))
            cp(srow_h[:, 1, :], srow_s).then_inc(s_srow, 1)
            chain(cp(loc_f[:, :], dst_i[:, :]))
            grouped = loc_f[:, :].rearrange("p (g k) -> p g k", k=GT)
            v.tensor_reduce(ext[:, 0, :], grouped, AX.X, ALU.max)
            chain(v.tensor_reduce(ext[:, 1, :], grouped, AX.X, ALU.min))
            v.tensor_scalar(ext[:, 1, :], ext[:, 1, :], -1.0, None, ALU.mult).then_inc(s_ext, 1)
            dve.wait_ge(s_const, 1)
            cp(iota_f[:, :], iota_i[:, :])
            cp(iota_h[:, :], iota_i[:, :])
            cp(pcol[:, :], pcol_i[:, :])
            cp(tnum[:, :], tnum_i[:, :])
            chain(v.tensor_scalar(pow_i[:, :], pow_i[:, :], 23, None, ALU.logical_shift_left))
            cp(pow_b[:, :], pow_i[:, :].bitcast(f32))
            v.tensor_scalar(thr[:, :], pow_i[:, :].bitcast(f32), 2.5, None, ALU.mult)
            v.tensor_scalar(dumpcol[:, :], pcol[:, :], float(DUMP), None, ALU.add)
            v.tensor_scalar(base[:, :], iota_f[:, 0:E], float(ROWS), None, ALU.mult)
            v.tensor_scalar(tok[:, :], iota_f[:, 0:TG], float(P), None, ALU.mult)
            chain(cp(src_f[:, :], src_i[:, :]))
            chain(v.tensor_scalar(tok[:, :], tok[:, :], pcol[:, 0:1], None, ALU.add))
            dve.wait_ge(s_w12c, 1)
            for n in range(3):
                chain(cp(bsplit[:, n, :], b12[:, :]))
                if n < 2:
                    chain(v.tensor_tensor(b12[:, :], b12[:, :], bsplit[:, n, :], ALU.subtract))
            dve.sem_inc(s_bias, 1)
            dve.wait_ge(s_ar, 1)
            v.tensor_scalar(win_i[:, :], exta[:, 1, :], -1.0, None, ALU.mult)
            chain(v.tensor_tensor(far[:, :], exta[:, 0, :], exta[:, 1, :], ALU.add))
            chain(v.tensor_reduce(keep[:, 0:1], far[:, :], AX.X, ALU.max))
            chain(v.tensor_scalar(wide_f[:, :], keep[:, 0:1], float(P), None, ALU.is_ge))
            cp(wide_i[:, :], wide_f[:, :])
            v.tensor_tensor(grouped, grouped, exta[:, 1, :].unsqueeze(2).broadcast_to([P, EG, GT]), ALU.add)
            v.tensor_scalar(keep[:, 0:1], wide_f[:, :], -1.0, 1.0, ALU.mult, ALU.add)
            chain(v.tensor_tensor(keep[:, 1:2], wide_f[:, :], pcol[:, :], ALU.mult))
            v.tensor_scalar(loc_f[:, :], loc_f[:, :], keep[:, 0:1], keep[:, 1:2], ALU.mult, ALU.add)\
                .then_inc(s_edges, 1)

            def norms(src, n):
                for t in range(TG):
                    last = v.bn_stats(bst[:, t, :], src(t))
                chain(last)
                for t in range(TG):
                    last = v.bn_aggr(mv[:, t, :], bst[:, t, :])
                chain(last)
                v.tensor_scalar(mv[:, :, 1], mv[:, :, 1], EPS, None, ALU.add).then_inc(s_var, 1)
                dve.wait_ge(s_sd, n)
                chain(v.reciprocal(rstd[:, :], rstd[:, :]))

            def normed(out_, in_, t):
                return v.tensor_scalar(out_, in_, mv[:, t, 0:1], rstd[:, t:t + 1], ALU.subtract, ALU.mult)

            dve.wait_ge(s_x, 16 * NG)
            with dve.Fori(0, NG) as g:
                chain.enter(g, 3)
                tile = lambda t: x_all[:, ds(g * TG + t, 1), :].rearrange("p a c -> p (a c)")
                norms(tile, g + 1)
                for t in range(TG):
                    last = normed(tile(t), tile(t), t)
                last.then_inc(s_yn, 1)
                dve.wait_ge(s_yh, g + 1)
                v.scalar_tensor_tensor(y_all[:, ds(g * TG, TG), C:2 * C], x_all[:, ds(g * TG, TG), :], SY,
                                       y_all[:, ds(g * TG, TG), 0:C], ALU.mult, ALU.subtract).then_inc(s_yl, 1)
                chain.leave(NG)

            dve.wait_ge(s_init, INIT_ALL)
            def edge_groups(it):
                chain.enter(it, 2 * 3)
                for s in range(2):
                    g = it * 2 + s
                    if later(g * 2):
                        dve.wait_ge(s_sel, g * 2)
                    v.tensor_tensor(oneh, iota_h[:, :].unsqueeze(1).broadcast_to([P, GT, P]),
                                    loc_f[:, ds(g * GT, GT)].unsqueeze(2).broadcast_to([P, GT, P]),
                                    ALU.is_equal).then_inc(s_one, 1)
                    for q in range(2):
                        dve.wait_ge(s_bc, g * 2 + q + 1)
                        v.tensor_tensor(eqb[:, q, :].rearrange("p (k n) -> p k n", k=QT),
                                        ps[:, q, :].rearrange("p (k n) -> p k n", k=QT),
                                        src_f[:, ds(g * GT + q * QT, QT)].unsqueeze(2).broadcast_to([P, QT, P]),
                                        ALU.is_equal).then_inc(s_eq, 1)
                    if later(g):
                        dve.wait_ge(s_wh, g)
                    dve.wait_ge(s_sel, g * 2 + 2)
                    if later(g):
                        dve.wait_ge(s_free, g)
                    v.tensor_scalar(isdup, ps[:, 6, 0:GT], thr[:, 0:1], None, ALU.is_gt)
                    chain(v.tensor_scalar(away, src_f[:, ds(g * GT, GT)], -1.0, dumpcol[:, 0:1], ALU.mult, ALU.add))
                    chain(v.tensor_tensor(away, away, isdup, ALU.mult))
                    chain(v.tensor_tensor(away, away, src_f[:, ds(g * GT, GT)], ALU.add))
                    cp(eidx[:, s, :], away).then_inc(s_idx, 1)
                    dve.wait_ge(s_wh, g + 1)
                    v.scalar_tensor_tensor(WL[:, ds(g * WCH, WCH)], wstage[:, s, :], SW, WH[:, ds(g * WCH, WCH)],
                                           ALU.mult, ALU.subtract).then_inc(s_wl, 1)

            turns(dve, edge_groups, EG // 2)
            chain.leave(EG // 2)
            def over(col):
                return col.unsqueeze(2).broadcast_to([P, TG, E])

            def residual(g):
                dve.wait_ge(s_xr[g % 2], (g // 2 + 1) * 16)
                dve.wait_ge(s_z, (g + 1) * NP)
                z = ps[:, 2:6, :].rearrange("p b n -> p (b n)")[:, 0:TG * C].rearrange("p (t c) -> p t c", t=TG)
                v.tensor_tensor(xres[:, g % 2, :, :], z, xres[:, g % 2, :, :], ALU.add).then_inc(s_x2, 1)

            def statistics(g):
                dve.wait_ge(s_x2, g + 1)
                norms(lambda t: xres[:, g % 2, t, :], NG + g + 1)

            def normalize(g):
                if g:
                    dve.wait_ge(s_sth, g * 16)
                    dve.wait_ge(s_xt, g * NP)
                for t in range(TG):
                    normed(xhat[:, t, :], xres[:, g % 2, t, :], t).then_inc(s_xn, 1)

            def pick(g):
                dve.wait_ge(s_lg, (g + 1) * NP)
                logits = lambda t: ps[:, 6, t * E:(t + 1) * E]
                for t in range(TG):
                    last = v.max(mx[:, t, :], logits(t))
                chain(last)
                for t in range(TG):
                    last = v.max_index(mxi[:, t, :], mx[:, t, :], logits(t))
                chain(last)
                v.tensor_tensor(dif[:, :, :], mx[:, :, :], over(mx[:, :, 0]), ALU.subtract).then_inc(s_mx, 1)
                chain(cp(sel[:, :, :], mxi[:, :, 0:2].rearrange("p t k -> p k t")))
                for k in range(2):
                    last = v.tensor_tensor(oneh_e[:, k, :, :], iota_f[:, 0:E].unsqueeze(1).broadcast_to([P, TG, E]),
                                           over(sel[:, k, :]), ALU.is_equal)
                chain(last)
                v.tensor_tensor(picked[:, :, :], oneh_e[:, 0, :, :], oneh_e[:, 1, :, :], ALU.add).then_inc(s_pk, 1)

            def gates(g):
                dve.wait_ge(s_ex, g + 1)
                chain(v.tensor_reduce(prb[:, 0, :], exs[:, :, :], AX.X, ALU.add))
                chain(v.reciprocal(prb[:, 1, :], prb[:, 0, :]))
                v.tensor_tensor(prb[:, 2, :], exs[:, :, 1], prb[:, 1, :], ALU.mult)
                chain(v.tensor_tensor(prb[:, 1, :], exs[:, :, 0], prb[:, 1, :], ALU.mult))
                chain(v.tensor_tensor(prb[:, 3, :], prb[:, 1, :], prb[:, 2, :], ALU.add))
                chain(v.tensor_scalar(prb[:, 3, :], prb[:, 3, :], 1e-9, None, ALU.add))
                chain(v.reciprocal(prb[:, 0, :], prb[:, 3, :]))
                if g >= 2:
                    dve.wait_ge(s_scat[g % 2], g // 2 * 16 * 2 * TG)
                for k in range(2):
                    v.tensor_tensor(loadf[:, g % 2, :, k, 1], prb[:, 1 + k, :], prb[:, 0, :], ALU.mult)
                    last = cp(load_[:, g % 2, :, k, 0], tok[:, :])
                chain(last)
                chain(v.tensor_scalar(tok[:, :], tok[:, :], float(TG * P), None, ALU.add))

            def places(g):
                dve.wait_ge(s_rk, g + 1)
                chain(v.tensor_tensor(rank[:, :, :], ps[:, 7, 0:TG * E].rearrange("p (t e) -> p t e", e=E),
                                      base[:, :].unsqueeze(1).broadcast_to([P, TG, E]), ALU.add))
                v.tensor_tensor(base[:, :], ps[:, 7, 64:64 + E], base[:, :], ALU.add)
                for k in range(2):
                    last = v.tensor_tensor(prod[:, k, :, :], oneh_e[:, k, :, :], rank[:, :, :], ALU.mult)
                chain(last)
                for k in range(2):
                    last = v.tensor_reduce(place[:, k, :], prod[:, k, :, :], AX.X, ALU.add)
                chain(last)
                cp(place_i[:, g % 2, :, :], place[:, :, :]).then_inc(s_pos, 1)

            residual(0)
            statistics(0)
            normalize(0)
            pick(0)
            gates(0)
            places(0)
            for g in (1, 2):
                residual(g)
                statistics(g)
                if g == 1:
                    normalize(1)
            for g in range(1, NG):
                pick(g)
                if g + 1 < NG:
                    normalize(g + 1)
                gates(g)
                places(g)
                if g + 2 < NG:
                    residual(g + 2)
                    statistics(g + 2)

            dve.wait_ge(s_pos, NG)
            chain(v.tensor_scalar(cnt[:, :], iota_f[:, 0:E], -float(ROWS), float(P - 1), ALU.mult, ALU.add))
            chain(v.tensor_tensor(cnt[:, :], cnt[:, :], base[:, :], ALU.add))
            chain(cp(cnt_i[:, :], cnt[:, :]))
            chain(v.tensor_scalar(cnt_i[:, :], cnt_i[:, :], 7, None, ALU.logical_shift_right))
            chain(cp(ntl[:, :], cnt_i[:, :]))
            chain(v.tensor_scalar(jump[:, :], ntl[:, :], -float(P), float(ROWS), ALU.mult, ALU.add))
            chain(cp(tend[:, 0:1], ntl[:, 0:1]))
            for e in range(1, E):
                chain(v.tensor_tensor(tend[:, e:e + 1], tend[:, e - 1:e], ntl[:, e:e + 1], ALU.add))
            chain(v.memset(acc_e[:, :], 0.0))
            chain(v.tensor_scalar(acc_r[:, :], tnum[:, :], float(P), None, ALU.mult))
            for e in range(E - 1):
                chain(v.tensor_scalar(past[:, :], tnum[:, :], tend[:, e:e + 1], None, ALU.is_ge))
                v.tensor_tensor(acc_e[:, :], acc_e[:, :], past[:, :], ALU.add)
                chain(v.scalar_tensor_tensor(acc_r[:, :], past[:, :], jump[:, e:e + 1], acc_r[:, :], ALU.mult, ALU.add))
            cp(meta[:, 0, :], acc_r[:, :])
            v.tensor_scalar(meta[:, 1, :], acc_e[:, :], float(W13), None, ALU.mult)
            chain(v.tensor_scalar(meta[:, 2, :], acc_e[:, :], float(W2C), float(W2B), ALU.mult, ALU.add))
            v.memset(hb[:, H:KC * KH], 0.0).then_inc(s_meta, 1)

            def low_x(i, s):
                dve.wait_ge(a_x, i + 1)
                v.scalar_tensor_tensor(xTl[:, s, :, :], ps[:, 6, 0:C].rearrange("p (k n) -> p k n", k=2), SX,
                                       xTh[:, s, :, :],
                                       ALU.mult, ALU.subtract).then_inc(d_x, 1)

            def low_h(i):
                for c in range(2):
                    dve.wait_ge(a_t, i * 2 + c + 1)
                    if c == 0:
                        if later(i):
                            dve.wait_ge(p_y, i)
                    v.tensor_tensor(hTl[0:KH, 3 * c:3 * c + 3, :],
                                    ps[0:KH, 4 + c, 0:3 * P].rearrange("p (j n) -> p j n", j=3),
                                    hTh[0:KH, 3 * c:3 * c + 3, :], ALU.subtract).then_inc(d_t, 1)

            def gated(i, c):
                dve.wait_ge(a_s, i * 2 + c + 1)
                if later(i * 2):
                    dve.wait_ge(p_t, i * 2)
                v.scalar_tensor_tensor(hb[:, c * HC:(c + 1) * HC], ps[:, 2 * c + 1, 0:HC], SH / (SX * SW),
                                       sg[:, c, :], ALU.mult, ALU.mult).then_inc(d_h, 1)

            def weighed(i, s, turn):
                dve.wait_ge(p_y, i + 1)
                if later(i * 16):
                    dve.wait_ge(s_acc, i * 16)
                dve.wait_ge(s_slot[s], turn * 16 + 16)
                gate = slotsf[:, i, 1:2] if isinstance(i, int) else slotsf[:, ds(i, 1), 1]
                v.tensor_scalar(yg, ps[:, 7, 0:C], gate, 1.0 / (SH * SW), ALU.mult, ALU.mult).then_inc(d_y, 1)

            low_x(0, 0)
            gated(0, 0)
            low_x(1, 1)
            gated(0, 1)
            def tiles(it):
                for o in range(2):
                    i = it * 2 + 1 + o
                    low_h(i - 1)
                    gated(i, 0)
                    low_x(i + 1, o)
                    gated(i, 1)
                    weighed(i - 1, o, it)

            turns(dve, tiles, FT // 2)
            low_h(FT - 1)
            weighed(FT - 1, (FT - 1) % 2, FT // 2)


def kernel(**inputs):
    import numpy as np
    import concourse.bacc as bacc
    from concourse.bass_utils import run_bass_kernel_spmd

    a = {k: np.asarray(v) for k, v in inputs.items()}
    pad = np.pad
    src = pad(a["src"], (0, ET * P - EDGES), constant_values=DUMP)
    dst = pad(a["dst"], (0, ET * P - EDGES), constant_values=N - 1)
    w1, w3 = (a[n].transpose(0, 2, 1).reshape(E, 2, P, 2, 1, HC) for n in ("L0_ffn_w1", "L0_ffn_w3"))
    w13 = np.concatenate([w1, w3], axis=4).reshape(E * 2, P, 4 * HC).transpose(1, 0, 2).reshape(P, -1)
    w2 = pad(a["L0_ffn_w2"].transpose(0, 2, 1), ((0, 0), (0, KC * KH - H), (0, 0))).reshape(E * KC, KH, C)
    w2 = pad(w2, ((0, 0), (0, P - KH), (0, 0))).transpose(1, 0, 2).reshape(P, -1)
    wall = np.concatenate([w13, w2], axis=1).reshape(P, EG, WCH).transpose(1, 0, 2)
    arrays = {
        "x": pad(a["x"], ((0, ALLR - N), (0, 0))),
        "srcT": src.reshape(ET, P).T, "dstT": dst.reshape(ET, P).T, "src_rows": src.reshape(P, ET),
        "gw1t": a["L0_gnn_W1"].T, "gb1t": a["L0_gnn_b1"].reshape(GH // P, P).T,
        "gw2": a["L0_gnn_W2"], "gb2": a["L0_gnn_b2"].reshape(1, C),
        "rwt": a["L0_ffn_router_w"].T, "wall": wall,
    }
    arrays = {f"{k}_dram": np.ascontiguousarray(v) for k, v in arrays.items()}
    nc = bacc.Bacc("TRN2", target_bir_lowering=False, num_devices=1)
    args = [nc.dram_tensor(k, v.shape, mybir.dt.from_np(v.dtype), kind="ExternalInput").ap()
            for k, v in arrays.items()]
    out = nc.dram_tensor("out_dram", (ALLR, C), mybir.dt.float32, kind="ExternalOutput").ap()
    gnn_moe(nc, *args, out)
    r = run_bass_kernel_spmd(nc, [arrays], core_ids=[0])
    return r.results[0]["out_dram"][0:N]
```

```python
import concourse.bass as bass
from concourse import mybir
from contextlib import ExitStack

RMAX = bass.bass_isa.ReduceOp.max

P = 128
N, C, H, E = 6250, 256, 682, 8
GH = 512
NT = (N + P - 1) // P
ROWS = NT * P
DUMP = ROWS
ALLR = ROWS + P
EDGES = 106250
GT = 8
PT = 4
EG = (EDGES + P * GT - 1) // (P * GT)
ET = EG * GT
QT = 4
NCOPY = 4
TG = 7
NG = NT // TG
HB = 3
NP = (TG + 1) // 2
FT = (2 * ROWS + E * (P - 1)) // P
MT = FT + 3
DT = 4
TAB = (E - 1) * ROWS + MT * P
HC = 341
KC = (H + P - 1) // P
KR = H - (KC - 1) * P
W13 = 2 * 4 * HC
W2C = KC * C
W2B = E * W13
WCOLS = W2B + E * W2C
WCH = WCOLS // EG
SY, SX, SW, SH = 64.0, 64.0, 64.0, 4.0
EPS = 1e-5

assert NT == TG * NG and WCH * EG == WCOLS and EG % PT == 0 and (FT - 1) % DT == 0 and NG == 7 and KC == 6 and KR <= 64


def gnn_moe(nc, x, srcT, dstT, src_rows, gw1t, gb1t, gw2, gb2, rwt, wall, out):
    f32, f16, bf16 = mybir.dt.float32, mybir.dt.float16, mybir.dt.bfloat16
    i32, u32 = mybir.dt.int32, mybir.dt.uint32
    ALU, ACT, AX = mybir.AluOpType, mybir.ActivationFunctionType, mybir.AxisListType
    ds = bass.ds
    Offset = bass.IndirectOffsetOnAxis

    dram = lambda name, shape, dt: nc.dram_tensor(name, shape, dt).ap()
    agg = [dram(f"agg{r}", (ALLR, C), f32) for r in range(NCOPY)]
    yhl = dram("yhl", (ALLR, 2 * C), f16)
    xhat_d = dram("xhat_d", (ALLR, C), f32)
    srow_d = dram("srow_d", (2, ET * P), f16)
    table = dram("table", (TAB, 2), i32)
    tiled = lambda t: t.rearrange("(t p) c -> p t c", p=P)
    x_t, out_t, yhl_t, xhat_t = tiled(x), tiled(out), tiled(yhl), tiled(xhat_d)
    agg_t = [tiled(a) for a in agg]

    with ExitStack() as ctx:
        sb = lambda name, shape, dt: ctx.enter_context(nc.sbuf_tensor(name, shape, dt))
        sem = lambda name: ctx.enter_context(nc.semaphore(name))

        WH = sb("WH", [P, WCOLS], f16)
        WL = sb("WL", [P, WCOLS], f16)
        WHf = WH[:, :].bitcast(f32)
        x_all = WHf[:, 0:NT * C].rearrange("p (t c) -> p t c", c=C)
        zeros = WHf[:, NT * C:NT * C + 2560]
        y_all = WL[:, 0:NT * 2 * C].rearrange("p (t c) -> p t c", c=2 * C)
        WLi = WL[:, :].bitcast(i32)
        T0 = NT * C
        tab_init = WLi[:, T0:T0 + 2 * (TAB // P)].rearrange("p (t w) -> p t w", w=2)
        T1 = T0 + 2 * (TAB // P)
        srow_i = WLi[:, T1:T1 + ET]
        srow_s = WLi[:, T1 + ET:T1 + 2 * ET]
        srow_h = WL[:, 2 * (T1 + 2 * ET):2 * (T1 + 2 * ET) + 2 * ET].rearrange("p (w t) -> p w t", w=2)
        assert 2 * (T1 + 2 * ET) + 2 * ET <= WCOLS and NT * C + 2560 <= WCOLS // 2

        iota_i = sb("iota_i", [P, P], i32)
        iota_f = sb("iota_f", [P, P], f32)
        iota_h = sb("iota_h", [P, P], f16)
        pcol_i = sb("pcol_i", [P, 1], i32)
        pcol = sb("pcol", [P, 1], f32)
        ident = sb("ident", [P, P], f32)
        before = sb("before", [P, P], f16)
        ones_h = sb("ones_h", [P, P], f16)
        ones_r = sb("ones_r", [1, P], f32)
        ones_b = sb("ones_b", [3, P], bf16)
        mix = sb("mix", [2, P], f16)
        pow_i = sb("pow_i", [P, 1], i32)
        pow_b = sb("pow_b", [P, 1], bf16)
        thr = sb("thr", [P, 1], f32)
        dumpcol = sb("dumpcol", [P, 1], f32)

        src_i = sb("src_i", [P, ET], i32)
        src_f = sb("src_f", [P, ET], f32)
        dst_i = sb("dst_i", [P, ET], i32)
        loc_f = sb("loc_f", [P, ET], f32)
        ext = sb("ext", [P, 2, EG], f32)
        exta = sb("exta", [P, 2, EG], f32)
        far = sb("far", [P, EG], f32)
        keep = sb("keep", [P, 2], f32)
        win_i = sb("win_i", [P, EG], i32)
        wide_f = sb("wide_f", [P, 1], f32)
        wide_i = sb("wide_i", [P, 1], i32)

        w12 = sb("w12", [P, 2, C], f32)
        b12 = sb("b12", [1, C], f32)
        brows = sb("brows", [3, C], bf16)
        b1col = sb("b1col", [P, 4], f32)
        b2row = sb("b2row", [1, C], f32)
        rw_sb = sb("rw_sb", [P, 2, E], f32)

        ROOM = 11520
        room = sb("room", [P, ROOM], f32)
        cur = [0]

        def take(words, dt, pattern=None, **sizes):
            v = room[:, cur[0]:cur[0] + words]
            cur[0] += words
            assert cur[0] <= ROOM, cur[0]
            if dt != f32:
                v = v.bitcast(dt)
            return v.rearrange(pattern, **sizes) if pattern else v

        ybuf = take(2 * GT * C, f16, "p (s k c) -> p s k c", s=2, k=GT)
        obuf = take(2 * GT * C, f32, "p (s k c) -> p s k c", s=2, k=GT)
        srow = take(GT * P, f16, "p (s n) -> p s n", s=2)
        wstage = take(2 * WCH, f32, "p (s n) -> p s n", s=2)
        mv_a = wstage[:, 0, 0:2 * NT].rearrange("p (t w) -> p t w", w=2)
        rstd_a = wstage[:, 0, 2 * NT:3 * NT]
        eqb = take(QT * P, bf16, "p (q n) -> p q n", q=2)
        oneh = take(GT * P // 2, bf16, "p (k n) -> p k n", k=GT)
        msel = take(QT * P, f16, "p (q n) -> p q n", q=2)
        isdup = take(GT, f32)
        away = take(GT, f32)
        eidx = take(2 * GT, i32, "p (s k) -> p s k", s=2)
        gidx_b = take(1, i32)
        gw_a = room[:, 2 * GT * C:2 * GT * C + 8 * C].rearrange("p (j c) -> p j c", c=C)
        bsplit = obuf[0:1, 1, GT - 2:GT, :].rearrange("p k c -> p (k c)")[:, 0:3 * C // 2].bitcast(bf16)\
            .rearrange("p (n c) -> p n c", n=3)
        cur[0] = 0
        hsum = take(HB * TG * C, f32, "p (s t c) -> p s t c", s=HB, t=TG)
        xres = take(2 * TG * C, f32, "p (s t c) -> p s t c", s=2, t=TG)
        xhat = take(TG * C, f32, "p (t c) -> p t c", t=TG)
        pair = lambda t: t[:, 0:2 * C].rearrange("p (t k n) -> p t k n", t=2, k=2)
        first = [xhat, hsum[:, HB - 1, :, :], xres[:, 1, :, :]]
        xT = [pair(take(2 * C, f32)), pair(src_i[:, :].bitcast(f32))]
        hT = [pair(loc_f), pair(dst_i[:, :].bitcast(f32))]
        cur[0] = 0
        xg = take(2 * C, f32, "p (s c) -> p s c", s=2)
        xTh = take(C, f16, "p (s k n) -> p s k n", s=2, k=2)
        xTl = take(C, f16, "p (s k n) -> p s k n", s=2, k=2)
        sg = take(2 * HC, f32, "p (s n) -> p s n", s=2)
        hb = take(KC * P, f32)
        hTh = take(KC * P // 2, f16, "p (j n) -> p j n", j=KC)
        hTl = take(KC * P // 2, f16, "p (j n) -> p j n", j=KC)
        yg = take(C, f32)
        slots = take(2 * MT, i32, "p (i w) -> p i w", w=2)
        slotsf = slots.bitcast(f32)

        bst = sb("bst", [P, TG, 6], f32)
        mv = sb("mv", [P, TG, 2], f32)
        rstd = sb("rstd", [P, TG], f32)
        mx = sb("mx", [P, TG, 8], f32)
        mxi = sb("mxi", [P, TG, 8], u32)
        sel = sb("sel", [P, 2, TG], f32)
        dif = sb("dif", [P, TG, 8], f32)
        exs = sb("exs", [P, TG, 8], f32)
        prb = sb("prb", [P, 4, TG], f32)
        oneh_e = sb("oneh_e", [P, 2, TG, E], f32)
        picked = sb("picked", [P, TG, E], f16)
        rank = sb("rank", [P, TG, E], f32)
        prod = sb("prod", [P, 2, TG, E], f32)
        place = sb("place", [P, 2, TG], f32)
        place_i = sb("place_i", [P, 2, 2, TG], i32)
        base = sb("base", [P, E], f32)
        tok = sb("tok", [P, TG], f32)
        load_ = sb("load_", [P, 2, TG, 2, 2], i32)
        loadf = load_[:, :, :, :, :].bitcast(f32)
        cnt = sb("cnt", [P, E], f32)
        cnt_i = sb("cnt_i", [P, E], i32)
        ntl = sb("ntl", [P, E], f32)
        tend = sb("tend", [P, E], f32)
        jump = sb("jump", [P, E], f32)
        tnum_i = sb("tnum_i", [P, MT], i32)
        tnum = sb("tnum", [P, MT], f32)
        past, acc_e, acc_r = (src_f[:, k * MT:(k + 1) * MT] for k in range(3))
        meta = sb("meta", [P, 3, MT], i32)
        gidx = sb("gidx", [P, 2], i32)
        sidx = sb("sidx", [P, 1], i32)

        ps = ctx.enter_context(nc.psum_tensor("ps", [P, 8, 512], f32))

        s_in = sem("s_in")
        s_x = sem("s_x")
        s_gw = sem("s_gw")
        s_pool = sem("s_pool")
        s_zero = sem("s_zero")
        s_const = sem("s_const")
        s_dve = sem("s_dve")
        s_tab = sem("s_tab")
        s_srow = sem("s_srow")
        s_ext = sem("s_ext")
        s_ar = sem("s_ar")
        s_edges = sem("s_edges")
        s_w12 = sem("s_w12")
        s_w12c = sem("s_w12c")
        s_var = sem("s_var")
        s_sd = sem("s_sd")
        s_yn = sem("s_yn")
        s_yh = sem("s_yh")
        s_yl = sem("s_yl")
        s_init = sem("s_init")
        s_win = [sem(f"s_win{s}") for s in range(2)]
        s_row = [sem(f"s_row{s}") for s in range(2)]
        s_wst = [sem(f"s_wst{s}") for s in range(2)]
        s_bc = sem("s_bc")
        s_eq = sem("s_eq")
        s_one = sem("s_one")
        s_idx = sem("s_idx")
        s_sel = sem("s_sel")
        s_selc = sem("s_selc")
        s_o = sem("s_o")
        s_ob = sem("s_ob")
        s_wcp = sem("s_wcp")
        s_free = sem("s_free")
        s_fill = sem("s_fill")
        s_srd = sem("s_srd")
        s_add = [sem(f"s_add{r}") for r in range(NCOPY)]
        s_wh = sem("s_wh")
        s_wl = sem("s_wl")
        s_bias = sem("s_bias")
        s_bias3 = sem("s_bias3")
        s_h0 = [sem(f"s_h0{s}") for s in range(HB)]
        s_first = [sem(f"s_first{r}") for r in range(1, NCOPY)]
        s_sum0 = sem("s_sum0")
        s_h3 = [sem(f"s_h3{s}") for s in range(HB)]
        s_xr = [sem(f"s_xr{s}") for s in range(2)]
        s_ht = sem("s_ht")
        s_htc = sem("s_htc")
        s_z = sem("s_z")
        s_x2 = sem("s_x2")
        s_xn = sem("s_xn")
        s_xt = sem("s_xt")
        s_xtc = sem("s_xtc")
        s_lg = sem("s_lg")
        s_mx = sem("s_mx")
        s_ex = sem("s_ex")
        s_pk = sem("s_pk")
        s_rk = sem("s_rk")
        s_pos = sem("s_pos")
        s_scat = [sem(f"s_scat{s}") for s in range(2)]
        s_st = [sem(f"s_st{s}") for s in range(2)]
        s_sth = sem("s_sth")
        s_meta = sem("s_meta")
        s_slot = [sem(f"s_slot{s}") for s in range(2)]
        s_cp = sem("s_cp")
        s_xg = [sem(f"s_xg{s}") for s in range(2)]
        p_x = sem("p_x")
        a_x = sem("a_x")
        d_x = sem("d_x")
        p_h = sem("p_h")
        a_s = sem("a_s")
        d_h = sem("d_h")
        p_t = sem("p_t")
        a_t = sem("a_t")
        d_t = sem("d_t")
        p_y = sem("p_y")
        d_y = sem("d_y")
        s_acc = sem("s_acc")
        block = ctx.enter_context(nc.Block())

        ZW = 2560
        ZD = ALLR // P * C // ZW
        INIT_ALL = 16 * ((NCOPY - 2) * ZD + 4 + 1 + 2 * NG)
        FIRST = [n % (NCOPY - 1) for n in range(2 * GT - 1)] + [NCOPY - 1]

        def before_add(r, n):
            return 16 * (FIRST.count(r) - 2 * GT // NCOPY + n)

        assert (2 * GT + 1) // (NCOPY - 1) == ZD
        ADDED = [before_add(r, ET // NCOPY) for r in range(NCOPY)]

        def zero_t(r, k):
            return agg[r].rearrange("(p t) c -> p (t c)", p=P)[:, k * ZW:(k + 1) * ZW]

        def part(v, i, n=1):
            return v[:, i:i + n] if isinstance(i, int) else v[:, ds(i, n)]

        def apart(eng):
            eng.nop(nofuse=True)

        def later(value):
            return not isinstance(value, int) or value > 0

        def turns(eng, body, count):
            body(0)
            with eng.Fori(1, count) as turn:
                body(turn)

        class Chain:

            def __init__(self, eng, s):
                self.eng, self.s, self.n, self.turn, self.start, self.steps = eng, s, 0, 0, 0, 0

            def __call__(self, ins):
                ins.then_inc(self.s, 1)
                self.n += 1
                self.eng.wait_ge(self.s, self.turn * self.steps + self.n)
                if self.steps:
                    apart(self.eng)

            def enter(self, turn, steps):
                if not self.steps:
                    self.start = self.n
                self.turn, self.steps, self.n = turn, steps, self.start

            def leave(self, count):
                assert self.n - self.start == self.steps, self.n - self.start
                self.n, self.turn, self.steps = self.start + count * self.steps, 0, 0

        @block.sync
        def _(sp):
            sp.dma_start(src_i[:, :], srcT).then_inc(s_in, 16)
            sp.dma_start(dst_i[:, :], dstT).then_inc(s_in, 16)
            sp.dma_start(srow_i, src_rows).then_inc(s_in, 16)
            for g in range(NG):
                t = slice(g * TG, (g + 1) * TG)
                sp.dma_start(x_all[:, t, :], x_t[:, t, :]).then_inc(s_x, 16)
            sp.dma_start(gw_a[:, 0:4, :], gw1t.rearrange("(j p) c -> p j c", p=P)).then_inc(s_gw, 16)
            sp.dma_start(gw_a[:, 4:8, :], gw2.rearrange("(j p) c -> p j c", p=P)).then_inc(s_gw, 16)
            sp.dma_start(b1col[:, :], gb1t).then_inc(s_gw, 16)
            sp.dma_start(b2row[:, :], gb2).then_inc(s_gw, 16)
            sp.dma_start(rw_sb[:, :, :], rwt.rearrange("(k p) e -> p k e", p=P)).then_inc(s_gw, 16)

            sp.wait_ge(s_zero, 1)
            for r in range(1, NCOPY - 1):
                for k in range(ZD):
                    sp.dma_start(zero_t(r, k), zeros).then_inc(s_init, 16)
            for t in (agg[0], xhat_d, out):
                sp.dma_start(t[DUMP:ALLR, :], zeros[:, 0:C]).then_inc(s_init, 16)
            sp.dma_start(yhl[DUMP:ALLR, :], zeros[:, 0:C].bitcast(f16)).then_inc(s_init, 16)
            sp.wait_ge(s_tab, 1)
            sp.dma_start(table.rearrange("(p t) w -> p t w", p=P), tab_init).then_inc(s_init, 16)
            sp.wait_ge(s_srow, 1)
            sp.dma_start(srow_d.rearrange("w (p t) -> p w t", p=P), srow_h).then_inc(s_srd, 16)
            for g in range(NG):
                t = slice(g * TG, (g + 1) * TG)
                sp.wait_ge(s_yl, g + 1)
                sp.dma_start(agg_t[0][:, t, :], x_all[:, t, :]).then_inc(s_init, 16)
                sp.dma_start(yhl_t[:, t, :], y_all[:, t, :]).then_inc(s_init, 16)

            def row_load(g, s):
                sp.dma_start(srow[0:2, s, :], part(srow_d, g * GT * P, GT * P)).then_inc(s_row[s], 16)

            sp.wait_ge(s_srd, 16)
            for g in range(2):
                row_load(g, g)
            sp.wait_ge(s_init, INIT_ALL)
            sp.wait_ge(s_edges, 1)
            wide = sp.value_load(wide_i[0:1, 0:1], min_val=0, max_val=1)

            def group_loads(g, s):
                win = sp.value_load(part(win_i[0:1, :], g), min_val=0, max_val=N - 1)
                with sp.If(wide == 0):
                    sp.sem_inc(s_win[s], 16 * (GT - 1))
                    sp.dma_start(ybuf[:, s, 0, :], yhl[ds(win, P), :]).then_inc(s_win[s], 16)
                sp.dma_start(wstage[:, s, :], wall[g] if isinstance(g, int)
                             else wall[ds(g, 1), :, :].rearrange("a p n -> p (a n)")).then_inc(s_wst[s], 16)

            for g in range(2):
                group_loads(g, g)
            with sp.Fori(0, EG // 2 - 1) as it:
                for s in range(2):
                    g = it * 2 + s
                    sp.wait_ge(s_ob, g * 4 + 4)
                    apart(sp)
                    sp.wait_ge(s_wl, g + 1)
                    apart(sp)
                    row_load(g + 2, s)
                    group_loads(g + 2, s)

            for r in range(NCOPY):
                sp.wait_ge(s_add[r], ADDED[r])
            sp.wait_ge(s_wl, EG)

            def sum_load(g):
                if g >= HB:
                    sp.wait_ge(s_ht, (g - HB + 1) * NP)
                sp.dma_start(hsum[:, g % HB, :, :], agg_t[0][:, g * TG:(g + 1) * TG, :])\
                    .then_inc(s_h0[g % HB], 16)

            sum_load(0)
            for r in range(1, NCOPY):
                sp.dma_start(first[r - 1], agg_t[r][:, 0:TG, :]).then_inc(s_first[r - 1], 16)
            for g in range(NG):
                s, t = g % 2, slice(g * TG, (g + 1) * TG)
                if g == 1:
                    sp.wait_ge(s_sum0, 1)
                if g + 1 < NG:
                    sum_load(g + 1)
                if g >= 2:
                    sp.wait_ge(s_xn, (g - 1) * TG)
                    sp.wait_ge(s_st[s], g // 2 * 16)
                sp.dma_start(xres[:, s, :, :], x_t[:, t, :]).then_inc(s_xr[s], 16)

            sp.wait_ge(s_meta, 1)
            for s in range(2):
                sp.wait_ge(s_scat[s], 16 * 2 * TG * ((NG + 1 - s) // 2))
                sp.wait_ge(s_st[s], 16 * ((NG + 1 - s) // 2))
            sp.wait_ge(s_sth, 16 * NG)
            def slot_loads(it):
                for s in range(2):
                    i = it * 2 + s
                    row = sp.value_load(meta[0:1, 0, ds(i, 1)], min_val=0, max_val=TAB - P)
                    if later(it * 16):
                        sp.wait_ge(s_slot[s], it * 16)
                    apart(sp)
                    sp.dma_start(slots[:, ds(i, 1), :],
                                 table[ds(row, P), :].rearrange("(a p) w -> p a w", p=P)).then_inc(s_slot[s], 16)

            turns(sp, slot_loads, MT // 2)
            for s in range(2):
                sp.wait_ge(s_slot[s], MT // 2 * 16)
        @block.gpsimd
        def _(pool):
            chain = Chain(pool, s_pool)
            chain(pool.memset(zeros, 0.0))
            chain(pool.iota(tab_init, pattern=[[1, TAB // P], [0, 2]], base=0, channel_multiplier=TAB // P))
            chain(pool.memset(tab_init[:, :, 1:2], 0))
            pool.sem_inc(s_zero, 1)
            chain(pool.iota(iota_i[:, :], pattern=[[1, P]], base=0, channel_multiplier=0))
            chain(pool.iota(pcol_i[:, :], pattern=[[0, 1]], base=0, channel_multiplier=1))
            chain(pool.iota(tnum_i[:, :], pattern=[[1, MT]], base=0, channel_multiplier=0))
            chain(pool.iota(pow_i[:, :], pattern=[[0, 1]], base=127 + 63, channel_multiplier=-1))
            chain(pool.memset(ident[:, :], 0.0))
            chain(pool.affine_select(out=ident[:, :], in_=ident[:, :], compare_op=ALU.not_equal, fill=1.0,
                                     base=0, pattern=[[-1, P]], channel_multiplier=1))
            chain(pool.memset(ones_h[:, :], 1.0))
            chain(pool.affine_select(out=before[:, :], in_=ones_h[:, :], compare_op=ALU.is_gt, fill=0.0,
                                     base=0, pattern=[[1, P]], channel_multiplier=-1))
            chain(pool.memset(ones_r[:, :], 1.0))
            chain(pool.memset(ones_b[:, :], 1.0))
            chain(pool.memset(mix[:, :], 1.0))
            chain(pool.memset(mix[0:1, :], 64.0))
            pool.sem_inc(s_const, 1)
            pool.wait_ge(s_ext, 1)
            pool.partition_all_reduce(exta[:, :, :].rearrange("p a g -> p (a g)"),
                                      ext[:, :, :].rearrange("p a g -> p (a g)"), P, RMAX).then_inc(s_ar, 1)

            pool.wait_ge(s_init, INIT_ALL)
            pool.wait_ge(s_edges, 1)
            wide = pool.value_load(wide_i[0:1, 0:1], min_val=0, max_val=1)
            def edge_groups(it):
                for u in range(PT):
                    s, g, pairs = u % 2, it * PT + u, it * (PT // 2) + u // 2
                    with pool.If(wide == 1):
                        if later(g * 4):
                            pool.wait_ge(s_ob, g * 4)
                        for k in range(GT):
                            if later((pairs * GT + k) * 16):
                                pool.wait_ge(s_win[s], (pairs * GT + k) * 16)
                            pool.tensor_copy(gidx_b, dst_i[:, ds(g * GT + k, 1)]).then_inc(s_wcp, 1)
                            pool.wait_ge(s_wcp, g * GT + k + 1)
                            apart(pool)
                            pool.indirect_dma_start(ybuf[:, s, k, :], None, yhl[:, :],
                                                    Offset(ap=gidx_b, axis=0)).then_inc(s_win[s], 16)
                        pool.wait_ge(s_win[s], (pairs + 1) * GT * 16)
                    pool.wait_ge(s_idx, g + 1)
                    for k in range(GT):
                        if k % 2 == 0:
                            pool.wait_ge(s_ob, g * 4 + k // 2 + 1)
                        if isinstance(it, int) and u < 2:
                            n = g * GT + k
                            r = FIRST[n]
                            if n % (NCOPY - 1) == 1:
                                pool.dma_start(zero_t(NCOPY - 1, n // (NCOPY - 1)), zeros).then_inc(s_fill, 16)
                            if r == NCOPY - 1:
                                pool.wait_ge(s_fill, 16 * ZD)
                            done = 16 * FIRST[:n].count(r)
                        else:
                            r = k % NCOPY
                            done = before_add(r, g * (GT // NCOPY) + k // NCOPY)
                        if later(done):
                            pool.wait_ge(s_add[r], done)
                        apart(pool)
                        pool.indirect_dma_start(agg[r][:, :], Offset(ap=eidx[:, s, k:k + 1], axis=0),
                                                obuf[:, s, k, :], None, bounds_check=ALLR - 1, oob_is_err=True,
                                                compute_op=ALU.add).then_inc(s_add[r], 16)
                        if k == NCOPY - 1:
                            pool.sem_inc(s_free, 1)

            turns(pool, edge_groups, EG // PT)
            for r in range(NCOPY):
                pool.wait_ge(s_add[r], ADDED[r])

            def add_copy(g, r):
                s = g % HB
                before = g // HB * (NCOPY - 1) + r - 1 - (NCOPY - 1) * (s == 0)
                if r == 1:
                    pool.wait_ge(s_h0[s], g // HB * 16 + 16)
                else:
                    pool.wait_ge(s_h3[s], before * 16)
                pool.dma_start(hsum[:, s, :, :], agg_t[r][:, g * TG:(g + 1) * TG, :],
                               accum_op=ALU.add).then_inc(s_h3[s], 16)

            for groups in ((1,), (2, 3)):
                for r in range(1, NCOPY):
                    for g in groups:
                        add_copy(g, r)
            for g in range(NG):
                pool.wait_ge(s_pos, g + 1)
                for t in range(TG):
                    for k in range(2):
                        pool.indirect_dma_start(table[:, :], Offset(ap=place_i[:, g % 2, k, t:t + 1], axis=0),
                                                load_[:, g % 2, t, k, :], None).then_inc(s_scat[g % 2], 16)
                    if g + HB + 1 < NG and t in (0, 3, 6):
                        add_copy(g + HB + 1, 1 + t // 3)

            def fetch(i, s, seen, done, copies):
                pool.wait_ge(s_slot[s], seen)
                if later(done):
                    pool.wait_ge(p_x, done)
                apart(pool)
                pool.tensor_copy(gidx[:, s:s + 1], slots[:, i, 0:1] if isinstance(i, int)
                                 else slots[:, ds(i, 1), 0]).then_inc(s_cp, 1)
                pool.wait_ge(s_cp, copies)
                apart(pool)
                pool.indirect_dma_start(xg[:, s, :], None, xhat_d[:, :],
                                        Offset(ap=gidx[:, s:s + 1], axis=0)).then_inc(s_xg[s], 16)

            def add_out(i, copies):
                if later(i * 16):
                    pool.wait_ge(s_acc, i * 16)
                apart(pool)
                pool.tensor_copy(sidx[:, :], slots[:, i, 0:1] if isinstance(i, int)
                                 else slots[:, ds(i, 1), 0]).then_inc(s_cp, 1)
                pool.wait_ge(s_cp, copies)
                pool.wait_ge(d_y, i + 1)
                apart(pool)
                pool.indirect_dma_start(out[:, :], Offset(ap=sidx[:, :], axis=0), yg, None,
                                        bounds_check=ALLR - 1, oob_is_err=True,
                                        compute_op=ALU.add).then_inc(s_acc, 16)

            pool.wait_ge(s_sth, 16 * NG)
            for s in range(2):
                pool.wait_ge(s_st[s], 16 * ((NG + 1 - s) // 2))
            for i in range(3):
                fetch(i, i % 2, i // 2 * 16 + 16, i - 1, i + 1)

            def tiles(it):
                for o in range(DT):
                    i = it * DT + 1 + o
                    fetch(i + 2, (1 + o) % 2, (it * (DT // 2) + (3 + o) // 2 + 1) * 16, i + 1,
                          it * (2 * DT) + 2 * o + 4)
                    add_out(i - 1, it * (2 * DT) + 2 * o + 5)

            turns(pool, tiles, FT // DT)
            add_out(FT - 1, 2 * FT + 2)
            pool.wait_ge(s_acc, 16 * FT)
            pool.wait_ge(s_xg[0], 16 * (FT // 2 + 2))
            pool.wait_ge(s_xg[1], 16 * (FT // 2 + 1))

        @block.tensor
        def _(pe):
            mm = nc.tensor.matmul

            pe.wait_ge(s_gw, 80)
            pe.wait_ge(s_const, 1)
            for k in range(2):
                for j in range(4):
                    mm(ps[:, k, 0:C], gw_a[:, j, k * P:(k + 1) * P], gw_a[:, 4 + j, :], start=j == 0, stop=j == 3)
            for j in range(4):
                mm(ps[0:1, 2, 0:C], b1col[:, j:j + 1], gw_a[:, 4 + j, :], start=j == 0, stop=False)
            mm(ps[0:1, 2, 0:C], ones_r[0:1, 0:1], b2row[:, :], start=False, stop=True).then_inc(s_w12, 1)
            pe.wait_ge(s_w12c, 1)

            pe.wait_ge(s_edges, 1)
            wide = pe.value_load(wide_i[0:1, 0:1], min_val=0, max_val=1)
            def edge_groups(it):
                for s in range(2):
                    g = it * 2 + s
                    pe.wait_ge(s_row[s], it * 16 + 16)
                    if later(g * 2):
                        pe.wait_ge(s_eq, g * 2)
                    for q in range(2):
                        mm(ps[:, q, :], mix[:, :], srow[0:2, s, q * QT * P:(q + 1) * QT * P],
                           start=True, stop=True).then_inc(s_bc, 1)
                    pe.wait_ge(s_one, g + 1)
                    if later(g):
                        pe.wait_ge(s_idx, g)
                    for q in range(2):
                        pe.wait_ge(s_eq, g * 2 + q + 1)
                        for k in range(QT):
                            e = eqb[:, q, k * P:(k + 1) * P]
                            mm(ps[:, 6, q * QT + k:q * QT + k + 1], e, pow_b[:, :], start=True, stop=True)
                        for k in range(QT):
                            e = eqb[:, q, k * P:(k + 1) * P]
                            last = mm(ps[:, 2 + q, k * P:(k + 1) * P], oneh[:, q * QT + k, :], e,
                                      start=True, stop=True)
                        last.then_inc(s_sel, 1)
                    pe.wait_ge(s_win[s], it * (16 * GT) + 16 * GT)
                    for j in range(GT // 2):
                        if j % 2 == 0:
                            pe.wait_ge(s_selc, g * 2 + j // 2 + 1)
                        if j >= 2:
                            pe.wait_ge(s_ob, g * 4 + j - 1)
                        for k in (2 * j, 2 * j + 1):
                            rows = ybuf[:, s, 0, :] if k == 0 else ybuf[:, s, ds(wide * k, 1), :]
                            m = msel[:, k // QT, (k % QT) * P:(k % QT + 1) * P]
                            for h in range(2):
                                y = rows[:, h * C:(h + 1) * C] if k == 0 else \
                                    rows[:, :, h * C:(h + 1) * C].rearrange("p a c -> p (a c)")
                                last = mm(ps[:, 4 + j % 2, (k % 2) * C:(k % 2 + 1) * C], m, y,
                                          start=h == 0, stop=h == 1)
                        last.then_inc(s_o, 1)

            turns(pe, edge_groups, EG // 2)
            def pair_of(j):
                return range(2 * j, min(2 * j + 2, TG))

            turned_to = [0]

            def gnn_out(g, pairs, ahead=True):
                def turn_sums(j):
                    n = g * NP + j
                    turned_to[0] = n + 1
                    if n >= 2:
                        pe.wait_ge(s_htc, n - 1)
                    for i, t in enumerate(pair_of(j)):
                        for k in range(2):
                            last = nc.tensor.transpose(ps[:, n % 2, (2 * i + k) * P:(2 * i + k + 1) * P],
                                                       hsum[:, g % HB, t, k * P:(k + 1) * P], ident[:, :])
                    last.then_inc(s_ht, 1)

                if pairs[0] == 0:
                    if g == 0:
                        pe.wait_ge(s_sum0, 1)
                    else:
                        pe.wait_ge(s_h3[g % HB], (g // HB + (g % HB > 0)) * 16 * (NCOPY - 1))
                if turned_to[0] == g * NP + pairs[0]:
                    turn_sums(pairs[0])
                if pairs[0] == 0 and g:
                    pe.wait_ge(s_x2, g)
                for j in range(*pairs):
                    if j + 1 < (NP if ahead else pairs[1]):
                        turn_sums(j + 1)
                    n = g * NP + j
                    pe.wait_ge(s_htc, n + 1)
                    for i, t in enumerate(pair_of(j)):
                        z = ps[:, 2 + j, i * C:(i + 1) * C]
                        for k in range(2):
                            mm(z, hT[n % 2][:, i, k, :], w12[:, k, :], start=k == 0, stop=False)
                        last = mm(z, ones_b[:, :], brows[:, :], start=False, stop=True)
                    last.then_inc(s_z, 1)

            def router(g):
                if g:
                    pe.wait_ge(s_mx, g)

                def turn_x(j):
                    n = g * NP + j
                    if n >= 2:
                        pe.wait_ge(s_xtc, n - 1)
                    for i, t in enumerate(pair_of(j)):
                        pe.wait_ge(s_xn, g * TG + t + 1)
                        for k in range(2):
                            last = nc.tensor.transpose(ps[:, n % 2, (2 * i + k) * P:(2 * i + k + 1) * P],
                                                       xhat[:, t, k * P:(k + 1) * P], ident[:, :])
                    last.then_inc(s_xt, 1)

                turn_x(0)
                for j in range(NP):
                    if j + 1 < NP:
                        turn_x(j + 1)
                    n = g * NP + j
                    pe.wait_ge(s_xtc, n + 1)
                    for i, t in enumerate(pair_of(j)):
                        for k in range(2):
                            last = mm(ps[:, 6, t * E:(t + 1) * E], xT[n % 2][:, i, k, :], rw_sb[:, k, :],
                                      start=k == 0, stop=k == 1)
                    last.then_inc(s_lg, 1)

            def ranks(g):
                pe.wait_ge(s_pk, g + 1)
                if g:
                    pe.wait_ge(s_pos, g)
                flat = picked[:, :, :].rearrange("p t e -> p (t e)")
                mm(ps[:, 7, 0:TG * E], before[:, :], flat, start=True, stop=False, skip_group_check=True)
                for d in range(1, TG):
                    mm(ps[:, 7, d * E:TG * E], ones_h[:, :], flat[:, 0:(TG - d) * E], start=False,
                       stop=d == TG - 1, skip_group_check=True)
                for t in range(TG):
                    last = mm(ps[:, 7, 64:64 + E], ones_h[:, :], picked[:, t, :], start=t == 0, stop=t == TG - 1)
                last.then_inc(s_rk, 1)

            pe.wait_ge(s_bias3, 16)
            gnn_out(0, (0, NP))
            gnn_out(1, (0, 2), False)
            router(0)
            gnn_out(1, (2, 3))
            ranks(0)
            gnn_out(1, (3, NP))
            gnn_out(2, (0, NP))
            router(1)
            for g in range(1, NG):
                if g + 2 < NG:
                    gnn_out(g + 2, (0, 1))
                ranks(g)
                if g + 2 < NG:
                    gnn_out(g + 2, (1, NP))
                if g + 1 < NG:
                    router(g + 1)

            def turn_tile(i, s, seen):
                pe.wait_ge(s_xg[s], seen)
                if later(i):
                    pe.wait_ge(d_x, i)
                for k in range(2):
                    last = nc.tensor.transpose(ps[:, 6, k * P:(k + 1) * P], xg[:, s, k * P:(k + 1) * P], ident[:, :])
                last.then_inc(p_x, 1)

            def hidden(i, s, halves, col, first):
                for c in halves:
                    if not first:
                        pe.wait_ge(d_h, i * 2 - 1 + c)
                    for k, (xp, wp) in enumerate(((xTh, WH), (xTh, WL), (xTl, WH))):
                        for kk in range(2):
                            for m in range(2):
                                o = kk * 4 * HC + c * 2 * HC + m * HC
                                last = mm(ps[:, 2 * c + m, 0:HC], xp[:, s, kk, :], wp[:, ds(col + o, HC)],
                                          start=k == 0 and kk == 0, stop=k == 2 and kk == 1)
                    last.then_inc(p_h, 1)

            def turn_h(i):
                pe.wait_ge(d_h, i * 2 + 2)
                if later(i * 2):
                    pe.wait_ge(d_t, i * 2)
                for j in range(KC):
                    last = nc.tensor.transpose(ps[:, 4 + j // 3, (j % 3) * P:(j % 3 + 1) * P],
                                               hb[:, j * P:(j + 1) * P], ident[:, :])
                    if j % 3 == 2:
                        last.then_inc(p_t, 1)

            def output(i, col):
                pe.wait_ge(d_t, i * 2 + 2)
                if later(i):
                    pe.wait_ge(d_y, i)
                for j in range(KC - 1):
                    for n, (hp, wp) in enumerate(((hTh, WH), (hTh, WL), (hTl, WH))):
                        mm(ps[:, 7, 0:C], hp[:, j, :], wp[:, ds(col + j * C, C)], start=j == 0 and n == 0, stop=False)
                j = KC - 1
                mm(ps[:, 7, 0:C], hTl[:, j, :], WH[:, ds(col + j * C, C)], start=False, stop=False)
                last = mm(ps[:, 7, 0:C], hTh[0:64, j, :], WL[0:64, ds(col + j * C, C)], start=False, stop=True)
                last.then_inc(p_y, 1)

            def column(row, i):
                v = meta[0:1, row, i:i + 1] if isinstance(i, int) else meta[0:1, row, ds(i, 1)]
                return pe.value_load(v, min_val=0 if row == 1 else W2B,
                                     max_val=(E - 1) * W13 if row == 1 else W2B + (E - 1) * W2C)

            pe.wait_ge(s_meta, 1)
            turn_tile(0, 0, 16)
            pe.wait_ge(d_x, 1)
            hidden(0, 0, (0,), column(1, 0), True)
            turn_tile(1, 1, 16)
            hidden(0, 0, (1,), column(1, 0), True)
            def tiles(it):
                for o in range(DT):
                    i = it * DT + 1 + o
                    w13, w2 = column(1, i), column(2, i - 1)
                    turn_h(i - 1)
                    pe.wait_ge(d_x, i + 1)
                    hidden(i, (1 + o) % 2, (0,), w13, False)
                    turn_tile(i + 1, o % 2, (it * (DT // 2) + (2 + o) // 2 + 1) * 16)
                    hidden(i, (1 + o) % 2, (1,), w13, False)
                    output(i - 1, w2)

            turns(pe, tiles, FT // DT)
            turn_h(FT - 1)
            output(FT - 1, column(2, FT - 1))

        @block.scalar
        def _(act):
            copy = lambda o, i, scale=1.0: nc.scalar.activation(o, i, ACT.Copy, scale=scale)
            act.wait_ge(s_w12, 1)
            copy(w12[:, :, :], ps[:, 0:2, 0:C])
            copy(b12[:, :], ps[0:1, 2, 0:C]).then_inc(s_w12c, 1)

            def roots(n, out_, in_):
                act.wait_ge(s_var, n)
                nc.scalar.activation(out_, in_, ACT.Sqrt).then_inc(s_sd, 1)

            roots(1, rstd_a, mv_a[:, :, 1])
            with act.Fori(0, NG) as g:
                act.wait_ge(s_yn, g + 1)
                copy(y_all[:, ds(g * TG, TG), 0:C], x_all[:, ds(g * TG, TG), :], SY).then_inc(s_yh, 1)

            act.wait_ge(s_bias, 1)
            act.dma_start(brows[:, :], bsplit).then_inc(s_bias3, 16)
            act.wait_ge(s_bias3, 16)

            def edge_groups(it):
                for s in range(2):
                    g = it * 2 + s
                    for q in range(2):
                        act.wait_ge(s_sel, g * 2 + q + 1)
                        copy(msel[:, q, :], ps[:, 2 + q, :]).then_inc(s_selc, 1)
                    if later(g):
                        act.wait_ge(s_free, g)
                    for j in range(GT // 2):
                        act.wait_ge(s_o, g * 4 + j + 1)
                        copy(obuf[:, s, 2 * j:2 * j + 2, :], ps[:, 4 + j % 2, :].rearrange("p (k c) -> p k c", k=2),
                             1.0 / SY).then_inc(s_ob, 1)
                    if isinstance(g, int):
                        act.wait_ge(s_init, INIT_ALL)
                    act.wait_ge(s_wst[s], it * 16 + 16)
                    copy(WH[:, ds(g * WCH, WCH)], wstage[:, s, :], SW).then_inc(s_wh, 1)

            turns(act, edge_groups, EG // 2)
            def turned(g, pairs, ready, read, out_, done):
                for j in range(*pairs):
                    n = g * NP + j
                    act.wait_ge(ready, n + 1)
                    if n >= 2:
                        act.wait_ge(read, n - 1)
                    w = min(2, TG - 2 * j)
                    copy(out_[n % 2][:, 0:w, :, :], ps[:, n % 2, 0:w * C]
                         .rearrange("p (t k n) -> p t k n", t=w, k=2)).then_inc(done, 1)

            def sums(g, pairs):
                turned(g, pairs, s_ht, s_z, hT, s_htc)

            def router_in(g, pairs):
                turned(g, pairs, s_xt, s_lg, xT, s_xtc)

            def store_x2(g):
                act.wait_ge(s_x2, g + 1)
                act.dma_start(out_t[:, g * TG:(g + 1) * TG, :], xres[:, g % 2, :, :]).then_inc(s_st[g % 2], 16)

            def store_xhat(g):
                act.dma_start(xhat_t[:, g * TG:(g + 1) * TG, :], xhat).then_inc(s_sth, 16)

            def exponentials(g):
                act.wait_ge(s_mx, g + 1)
                nc.scalar.activation(exs[:, :, :], dif[:, :, :], ACT.Exp).then_inc(s_ex, 1)

            sums(0, (0, NP))
            store_x2(0)
            sums(1, (0, 2))
            roots(2, rstd[:, :], mv[:, :, 1])
            router_in(0, (0, NP))
            store_xhat(0)
            sums(1, (2, 3))
            exponentials(0)
            sums(1, (3, NP))
            store_x2(1)
            sums(2, (0, 2))
            roots(3, rstd[:, :], mv[:, :, 1])
            sums(2, (2, NP))
            router_in(1, (0, 2))
            store_x2(2)
            router_in(1, (2, NP))
            roots(4, rstd[:, :], mv[:, :, 1])
            for g in range(1, NG):
                store_xhat(g)
                if g + 2 < NG:
                    sums(g + 2, (0, 1))
                exponentials(g)
                if g + 2 < NG:
                    sums(g + 2, (1, NP))
                if g + 1 < NG:
                    router_in(g + 1, (0, 2))
                if g + 2 < NG:
                    store_x2(g + 2)
                if g + 1 < NG:
                    router_in(g + 1, (2, NP))
                if g + 2 < NG:
                    roots(g + 4, rstd[:, :], mv[:, :, 1])

            def high_x(i, s):
                act.wait_ge(p_x, i + 1)
                if not isinstance(i, int) or i > 1:
                    act.wait_ge(p_h, i * 2 - 2)
                copy(xTh[:, s, :, :], ps[:, 6, 0:C].rearrange("p (k n) -> p k n", k=2), SX).then_inc(a_x, 1)

            def high_h(i):
                for c in range(2):
                    act.wait_ge(p_t, i * 2 + c + 1)
                    if c == 0:
                        if later(i):
                            act.wait_ge(p_y, i)
                    copy(hTh[:, 3 * c:3 * c + 3, :],
                         ps[:, 4 + c, 0:3 * P].rearrange("p (j n) -> p j n", j=3)).then_inc(a_t, 1)

            def silu(i, c, first=False):
                act.wait_ge(p_h, i * 2 + c + 1)
                if not first:
                    act.wait_ge(d_h, i * 2 - 1 + c)
                nc.scalar.activation(sg[:, c, :], ps[:, 2 * c, 0:HC], ACT.Silu,
                                     scale=1.0 / (SX * SW)).then_inc(a_s, 1)

            high_x(0, 0)
            silu(0, 0, True)
            high_x(1, 1)
            silu(0, 1, True)
            def tiles(it):
                for o in range(DT):
                    i = it * DT + 1 + o
                    high_h(i - 1)
                    silu(i, 0)
                    high_x(i + 1, o % 2)
                    silu(i, 1)

            turns(act, tiles, FT // DT)
            high_h(FT - 1)

        @block.vector
        def _(dve):
            v = nc.vector
            chain = Chain(dve, s_dve)
            cp = v.tensor_copy
            dve.wait_ge(s_zero, 1)
            t0 = tab_init[:, :, 0]
            chain(v.tensor_scalar(t0, t0, P - 1, None, ALU.bitwise_and))
            v.tensor_scalar(t0, t0, DUMP, None, ALU.add).then_inc(s_tab, 1)
            dve.wait_ge(s_in, 48)
            chain(v.tensor_scalar(srow_s, srow_i, 6, None, ALU.logical_shift_right))
            chain(cp(srow_h[:, 0, :], srow_s))
            chain(v.tensor_scalar(srow_s, srow_i, 63, None, ALU.bitwise_and))
            cp(srow_h[:, 1, :], srow_s).then_inc(s_srow, 1)
            chain(cp(loc_f[:, :], dst_i[:, :]))
            grouped = loc_f[:, :].rearrange("p (g k) -> p g k", k=GT)
            v.tensor_reduce(ext[:, 0, :], grouped, AX.X, ALU.max)
            chain(v.tensor_reduce(ext[:, 1, :], grouped, AX.X, ALU.min))
            v.tensor_scalar(ext[:, 1, :], ext[:, 1, :], -1.0, None, ALU.mult).then_inc(s_ext, 1)
            dve.wait_ge(s_const, 1)
            cp(iota_f[:, :], iota_i[:, :])
            cp(iota_h[:, :], iota_i[:, :])
            cp(pcol[:, :], pcol_i[:, :])
            cp(tnum[:, :], tnum_i[:, :])
            chain(v.tensor_scalar(pow_i[:, :], pow_i[:, :], 23, None, ALU.logical_shift_left))
            cp(pow_b[:, :], pow_i[:, :].bitcast(f32))
            v.tensor_scalar(thr[:, :], pow_i[:, :].bitcast(f32), 2.5, None, ALU.mult)
            v.tensor_scalar(dumpcol[:, :], pcol[:, :], float(DUMP), None, ALU.add)
            v.tensor_scalar(base[:, :], iota_f[:, 0:E], float(ROWS), None, ALU.mult)
            v.tensor_scalar(tok[:, :], iota_f[:, 0:TG], float(P), None, ALU.mult)
            chain(cp(src_f[:, :], src_i[:, :]))
            chain(v.tensor_scalar(tok[:, :], tok[:, :], pcol[:, 0:1], None, ALU.add))
            dve.wait_ge(s_ar, 1)
            v.tensor_scalar(win_i[:, :], exta[:, 1, :], -1.0, None, ALU.mult)
            chain(v.tensor_tensor(far[:, :], exta[:, 0, :], exta[:, 1, :], ALU.add))
            chain(v.tensor_reduce(keep[:, 0:1], far[:, :], AX.X, ALU.max))
            chain(v.tensor_scalar(wide_f[:, :], keep[:, 0:1], float(P), None, ALU.is_ge))
            cp(wide_i[:, :], wide_f[:, :])
            v.tensor_tensor(grouped, grouped, exta[:, 1, :].unsqueeze(2).broadcast_to([P, EG, GT]), ALU.add)
            v.tensor_scalar(keep[:, 0:1], wide_f[:, :], -1.0, 1.0, ALU.mult, ALU.add)
            chain(v.tensor_tensor(keep[:, 1:2], wide_f[:, :], pcol[:, :], ALU.mult))
            v.tensor_scalar(loc_f[:, :], loc_f[:, :], keep[:, 0:1], keep[:, 1:2], ALU.mult, ALU.add)\
                .then_inc(s_edges, 1)

            def norms(src, n):
                for t in range(TG):
                    last = v.bn_stats(bst[:, t, :], src(t))
                chain(last)
                for t in range(TG):
                    last = v.bn_aggr(mv[:, t, :], bst[:, t, :])
                chain(last)
                v.tensor_scalar(mv[:, :, 1], mv[:, :, 1], EPS, None, ALU.add).then_inc(s_var, 1)
                dve.wait_ge(s_sd, n)
                chain(v.reciprocal(rstd[:, :], rstd[:, :]))

            def normed(out_, in_, t):
                return v.tensor_scalar(out_, in_, mv[:, t, 0:1], rstd[:, t:t + 1], ALU.subtract, ALU.mult)

            dve.wait_ge(s_x, 16 * NG)
            tile = lambda t: x_all[:, ds(t, 1), :].rearrange("p a c -> p (a c)")
            with dve.Fori(0, NG) as g:
                chain.enter(g, 3)
                for t in range(TG):
                    last = v.bn_stats(bst[:, t, :], tile(g * TG + t))
                chain(last)
                for t in range(TG):
                    last = v.bn_aggr(mv[:, t, :], bst[:, t, :])
                chain(last)
                chain(cp(mv_a[:, ds(g * TG, TG), :], mv[:, :, :]))
                chain.leave(NG)
            v.tensor_scalar(mv_a[:, :, 1], mv_a[:, :, 1], EPS, None, ALU.add).then_inc(s_var, 1)
            dve.wait_ge(s_sd, 1)
            chain(v.reciprocal(rstd_a, rstd_a))

            def low_y(g):
                dve.wait_ge(s_yh, g + 1)
                t = ds(g * TG, TG)
                v.scalar_tensor_tensor(y_all[:, t, C:2 * C], x_all[:, t, :], SY, y_all[:, t, 0:C],
                                       ALU.mult, ALU.subtract).then_inc(s_yl, 1)

            def scale_y(g):
                for t in range(TG):
                    n = g * TG + t
                    last = v.tensor_scalar(tile(n), tile(n), mv_a[:, ds(n, 1), 0], rstd_a[:, ds(n, 1)],
                                           ALU.subtract, ALU.mult)
                last.then_inc(s_yn, 1)
                if later(g):
                    low_y(g - 1)

            turns(dve, scale_y, NG)
            low_y(NG - 1)
            dve.wait_ge(s_w12c, 1)
            for n in range(3):
                chain(cp(bsplit[:, n, :], b12[:, :]))
                if n < 2:
                    chain(v.tensor_tensor(b12[:, :], b12[:, :], bsplit[:, n, :], ALU.subtract))
            dve.sem_inc(s_bias, 1)

            def edge_groups(it):
                chain.enter(it, 2 * 3)
                for s in range(2):
                    g = it * 2 + s
                    if later(g * 2):
                        dve.wait_ge(s_sel, g * 2)
                    v.tensor_tensor(oneh, iota_h[:, :].unsqueeze(1).broadcast_to([P, GT, P]),
                                    loc_f[:, ds(g * GT, GT)].unsqueeze(2).broadcast_to([P, GT, P]),
                                    ALU.is_equal).then_inc(s_one, 1)
                    for q in range(2):
                        dve.wait_ge(s_bc, g * 2 + q + 1)
                        v.tensor_tensor(eqb[:, q, :].rearrange("p (k n) -> p k n", k=QT),
                                        ps[:, q, :].rearrange("p (k n) -> p k n", k=QT),
                                        src_f[:, ds(g * GT + q * QT, QT)].unsqueeze(2).broadcast_to([P, QT, P]),
                                        ALU.is_equal).then_inc(s_eq, 1)
                    if later(g):
                        dve.wait_ge(s_wh, g)
                    dve.wait_ge(s_sel, g * 2 + 2)
                    if later(g):
                        dve.wait_ge(s_free, g)
                    v.tensor_scalar(isdup, ps[:, 6, 0:GT], thr[:, 0:1], None, ALU.is_gt)
                    chain(v.tensor_scalar(away, src_f[:, ds(g * GT, GT)], -1.0, dumpcol[:, 0:1], ALU.mult, ALU.add))
                    chain(v.tensor_tensor(away, away, isdup, ALU.mult))
                    chain(v.tensor_tensor(away, away, src_f[:, ds(g * GT, GT)], ALU.add))
                    cp(eidx[:, s, :], away).then_inc(s_idx, 1)
                    if isinstance(g, int):
                        dve.wait_ge(s_init, INIT_ALL)
                    dve.wait_ge(s_wh, g + 1)
                    v.scalar_tensor_tensor(WL[:, ds(g * WCH, WCH)], wstage[:, s, :], SW, WH[:, ds(g * WCH, WCH)],
                                           ALU.mult, ALU.subtract).then_inc(s_wl, 1)

            turns(dve, edge_groups, EG // 2)
            chain.leave(EG // 2)
            def over(col):
                return col.unsqueeze(2).broadcast_to([P, TG, E])

            def residual(g):
                dve.wait_ge(s_xr[g % 2], (g // 2 + 1) * 16)
                dve.wait_ge(s_z, (g + 1) * NP)
                z = ps[:, 2:6, :].rearrange("p b n -> p (b n)")[:, 0:TG * C].rearrange("p (t c) -> p t c", t=TG)
                v.tensor_tensor(xres[:, g % 2, :, :], z, xres[:, g % 2, :, :], ALU.add).then_inc(s_x2, 1)

            def statistics(g):
                dve.wait_ge(s_x2, g + 1)
                norms(lambda t: xres[:, g % 2, t, :], g + 2)

            def normalize(g):
                if g:
                    dve.wait_ge(s_sth, g * 16)
                    dve.wait_ge(s_xt, g * NP)
                for t in range(TG):
                    normed(xhat[:, t, :], xres[:, g % 2, t, :], t).then_inc(s_xn, 1)

            def pick(g):
                dve.wait_ge(s_lg, (g + 1) * NP)
                logits = lambda t: ps[:, 6, t * E:(t + 1) * E]
                for t in range(TG):
                    last = v.max(mx[:, t, :], logits(t))
                chain(last)
                for t in range(TG):
                    last = v.max_index(mxi[:, t, :], mx[:, t, :], logits(t))
                chain(last)
                v.tensor_tensor(dif[:, :, :], mx[:, :, :], over(mx[:, :, 0]), ALU.subtract).then_inc(s_mx, 1)
                chain(cp(sel[:, :, :], mxi[:, :, 0:2].rearrange("p t k -> p k t")))
                for k in range(2):
                    last = v.tensor_tensor(oneh_e[:, k, :, :], iota_f[:, 0:E].unsqueeze(1).broadcast_to([P, TG, E]),
                                           over(sel[:, k, :]), ALU.is_equal)
                chain(last)
                v.tensor_tensor(picked[:, :, :], oneh_e[:, 0, :, :], oneh_e[:, 1, :, :], ALU.add).then_inc(s_pk, 1)

            def gates(g):
                dve.wait_ge(s_ex, g + 1)
                chain(v.tensor_reduce(prb[:, 0, :], exs[:, :, :], AX.X, ALU.add))
                chain(v.reciprocal(prb[:, 1, :], prb[:, 0, :]))
                v.tensor_tensor(prb[:, 2, :], exs[:, :, 1], prb[:, 1, :], ALU.mult)
                chain(v.tensor_tensor(prb[:, 1, :], exs[:, :, 0], prb[:, 1, :], ALU.mult))
                chain(v.tensor_tensor(prb[:, 3, :], prb[:, 1, :], prb[:, 2, :], ALU.add))
                chain(v.tensor_scalar(prb[:, 3, :], prb[:, 3, :], 1e-9, None, ALU.add))
                chain(v.reciprocal(prb[:, 0, :], prb[:, 3, :]))
                if g >= 2:
                    dve.wait_ge(s_scat[g % 2], g // 2 * 16 * 2 * TG)
                for k in range(2):
                    v.tensor_tensor(loadf[:, g % 2, :, k, 1], prb[:, 1 + k, :], prb[:, 0, :], ALU.mult)
                    last = cp(load_[:, g % 2, :, k, 0], tok[:, :])
                chain(last)
                chain(v.tensor_scalar(tok[:, :], tok[:, :], float(TG * P), None, ALU.add))

            def places(g):
                dve.wait_ge(s_rk, g + 1)
                chain(v.tensor_tensor(rank[:, :, :], ps[:, 7, 0:TG * E].rearrange("p (t e) -> p t e", e=E),
                                      base[:, :].unsqueeze(1).broadcast_to([P, TG, E]), ALU.add))
                v.tensor_tensor(base[:, :], ps[:, 7, 64:64 + E], base[:, :], ALU.add)
                for k in range(2):
                    last = v.tensor_tensor(prod[:, k, :, :], oneh_e[:, k, :, :], rank[:, :, :], ALU.mult)
                chain(last)
                for k in range(2):
                    last = v.tensor_reduce(place[:, k, :], prod[:, k, :, :], AX.X, ALU.add)
                chain(last)
                cp(place_i[:, g % 2, :, :], place[:, :, :]).then_inc(s_pos, 1)

            dve.wait_ge(s_h0[0], 16)
            for r in range(1, NCOPY):
                dve.wait_ge(s_first[r - 1], 16)
                last = v.tensor_tensor(hsum[:, 0, :, :], hsum[:, 0, :, :], first[r - 1], ALU.add)
                if r < NCOPY - 1:
                    chain(last)
            last.then_inc(s_sum0, 1)
            residual(0)
            statistics(0)
            normalize(0)
            pick(0)
            gates(0)
            places(0)
            for g in (1, 2):
                residual(g)
                statistics(g)
                if g == 1:
                    normalize(1)
            for g in range(1, NG):
                pick(g)
                gates(g)
                places(g)
                if g + 1 < NG:
                    normalize(g + 1)
                if g + 2 < NG:
                    residual(g + 2)
                    statistics(g + 2)

            dve.wait_ge(s_pos, NG)
            chain(v.tensor_scalar(cnt[:, :], iota_f[:, 0:E], -float(ROWS), float(P - 1), ALU.mult, ALU.add))
            chain(v.tensor_tensor(cnt[:, :], cnt[:, :], base[:, :], ALU.add))
            chain(cp(cnt_i[:, :], cnt[:, :]))
            chain(v.tensor_scalar(cnt_i[:, :], cnt_i[:, :], 7, None, ALU.logical_shift_right))
            chain(cp(ntl[:, :], cnt_i[:, :]))
            chain(v.tensor_scalar(jump[:, :], ntl[:, :], -float(P), float(ROWS), ALU.mult, ALU.add))
            chain(cp(tend[:, 0:1], ntl[:, 0:1]))
            for e in range(1, E):
                chain(v.tensor_tensor(tend[:, e:e + 1], tend[:, e - 1:e], ntl[:, e:e + 1], ALU.add))
            chain(v.memset(acc_e[:, :], 0.0))
            chain(v.tensor_scalar(acc_r[:, :], tnum[:, :], float(P), None, ALU.mult))
            for e in range(E - 1):
                chain(v.tensor_scalar(past[:, :], tnum[:, :], tend[:, e:e + 1], None, ALU.is_ge))
                v.tensor_tensor(acc_e[:, :], acc_e[:, :], past[:, :], ALU.add)
                chain(v.scalar_tensor_tensor(acc_r[:, :], past[:, :], jump[:, e:e + 1], acc_r[:, :], ALU.mult, ALU.add))
            cp(meta[:, 0, :], acc_r[:, :])
            v.tensor_scalar(meta[:, 1, :], acc_e[:, :], float(W13), None, ALU.mult)
            chain(v.tensor_scalar(meta[:, 2, :], acc_e[:, :], float(W2C), float(W2B), ALU.mult, ALU.add))
            v.memset(hb[:, H:KC * P], 0.0).then_inc(s_meta, 1)

            def low_x(i, s):
                dve.wait_ge(a_x, i + 1)
                v.scalar_tensor_tensor(xTl[:, s, :, :], ps[:, 6, 0:C].rearrange("p (k n) -> p k n", k=2), SX,
                                       xTh[:, s, :, :],
                                       ALU.mult, ALU.subtract).then_inc(d_x, 1)

            def low_h(i):
                for c in range(2):
                    dve.wait_ge(a_t, i * 2 + c + 1)
                    if c == 0:
                        if later(i):
                            dve.wait_ge(p_y, i)
                    w = 3 - c
                    last = v.tensor_tensor(hTl[:, 3 * c:3 * c + w, :],
                                           ps[:, 4 + c, 0:w * P].rearrange("p (j n) -> p j n", j=w),
                                           hTh[:, 3 * c:3 * c + w, :], ALU.subtract)
                    if c == 1:
                        cp(hTl[0:64, KC - 1, :], hTh[0:64, KC - 1, :])
                        last = v.tensor_tensor(hTl[64:P, KC - 1, :], ps[64:P, 5, 2 * P:3 * P], hTh[64:P, KC - 1, :],
                                               ALU.subtract)
                    last.then_inc(d_t, 1)

            def gated(i, c):
                dve.wait_ge(a_s, i * 2 + c + 1)
                if later(i * 2):
                    dve.wait_ge(p_t, i * 2)
                last = v.scalar_tensor_tensor(hb[:, c * HC:(c + 1) * HC], ps[:, 2 * c + 1, 0:HC], SH / (SX * SW),
                                              sg[:, c, :], ALU.mult, ALU.mult)
                if c == 1:
                    last = v.scalar_tensor_tensor(hb[:, H - KR + 64:H + 64], ps[:, 3, HC - KR:HC], SH / (SX * SW),
                                                  sg[:, 1, HC - KR:HC], ALU.mult, ALU.mult)
                last.then_inc(d_h, 1)

            def weighed(i, s, turn):
                dve.wait_ge(p_y, i + 1)
                if later(i * 16):
                    dve.wait_ge(s_acc, i * 16)
                dve.wait_ge(s_slot[s], turn * 16 + 16)
                gate = slotsf[:, i, 1:2] if isinstance(i, int) else slotsf[:, ds(i, 1), 1]
                v.tensor_scalar(yg, ps[:, 7, 0:C], gate, 1.0 / (SH * SW), ALU.mult, ALU.mult).then_inc(d_y, 1)

            low_x(0, 0)
            gated(0, 0)
            low_x(1, 1)
            gated(0, 1)
            def tiles(it):
                for o in range(DT):
                    i = it * DT + 1 + o
                    low_h(i - 1)
                    gated(i, 0)
                    low_x(i + 1, o % 2)
                    gated(i, 1)
                    weighed(i - 1, o % 2, it * (DT // 2) + o // 2)

            turns(dve, tiles, FT // DT)
            low_h(FT - 1)
            weighed(FT - 1, (FT - 1) % 2, FT // 2)


def kernel(**inputs):
    import numpy as np
    import concourse.bacc as bacc
    from concourse.bass_utils import run_bass_kernel_spmd

    a = {k: np.asarray(v) for k, v in inputs.items()}
    pad = np.pad
    src = pad(a["src"], (0, ET * P - EDGES), constant_values=DUMP)
    dst = pad(a["dst"], (0, ET * P - EDGES), constant_values=N - 1)
    w1, w3 = (a[n].transpose(0, 2, 1).reshape(E, 2, P, 2, 1, HC) for n in ("L0_ffn_w1", "L0_ffn_w3"))
    w13 = np.concatenate([w1, w3], axis=4).reshape(E * 2, P, 4 * HC).transpose(1, 0, 2).reshape(P, -1)
    w2 = pad(a["L0_ffn_w2"].transpose(0, 2, 1), ((0, 0), (0, KC * P - H), (0, 0)))
    w2[:, H - KR + 64:H + 64] = w2[:, H - KR:H]
    w2 = w2.reshape(E * KC, P, C).transpose(1, 0, 2).reshape(P, -1)
    wall = np.concatenate([w13, w2], axis=1).reshape(P, EG, WCH).transpose(1, 0, 2)
    arrays = {
        "x": pad(a["x"], ((0, ALLR - N), (0, 0))),
        "srcT": src.reshape(ET, P).T, "dstT": dst.reshape(ET, P).T, "src_rows": src.reshape(P, ET),
        "gw1t": a["L0_gnn_W1"].T, "gb1t": a["L0_gnn_b1"].reshape(GH // P, P).T,
        "gw2": a["L0_gnn_W2"], "gb2": a["L0_gnn_b2"].reshape(1, C),
        "rwt": a["L0_ffn_router_w"].T, "wall": wall,
    }
    arrays = {f"{k}_dram": np.ascontiguousarray(v) for k, v in arrays.items()}
    nc = bacc.Bacc("TRN2", target_bir_lowering=False, num_devices=1)
    args = [nc.dram_tensor(k, v.shape, mybir.dt.from_np(v.dtype), kind="ExternalInput").ap()
            for k, v in arrays.items()]
    out = nc.dram_tensor("out_dram", (ALLR, C), mybir.dt.float32, kind="ExternalOutput").ap()
    gnn_moe(nc, *args, out)
    r = run_bass_kernel_spmd(nc, [arrays], core_ids=[0])
    return r.results[0]["out_dram"][0:N]
```
